# Optimizing a Trainium2 kernel written in Bass

```python
import numpy as np
import jax
import jax.numpy as jnp

def _softmax(x, axis=-1):
    return jax.nn.softmax(x, axis=axis)

def _gelu(x):
    return jax.nn.gelu(x, approximate=True)

def _silu(x):
    return jax.nn.silu(x)

def _sigmoid(x):
    return jax.nn.sigmoid(x)

def _layernorm(x, axis=-1, eps=1e-05):
    m = jnp.mean(x, axis=axis, keepdims=True)
    v = jnp.var(x, axis=axis, keepdims=True)
    return (x - m) / jnp.sqrt(v + eps)

def _scatter_add(tgt, idx, src, axis=0):
    return tgt.at[idx].add(src)

def _segment_sum(src, seg, n):
    return jax.ops.segment_sum(src, seg, n)
kernel_name = 'mk_xattn_ffn_d1_seqx_r4_90013c'

def setup_inputs(seed: int=0):
    np.random.seed(seed)
    _w = jnp.asarray

    def _rec_inputs():
        import jax
        import jax.numpy as jnp
        _rk = jax.random.key(seed)
        x = -0.000125 + 0.9999 * jax.random.normal(jax.random.fold_in(_rk, 1), (4, 512, 512), jnp.float32)
        _lenS = 512 - jax.random.randint(jax.random.fold_in(_rk, 7), (4,), 0, max(1, 512 // 4) + 1, jnp.int32)
        _lenS2 = 512 - jax.random.randint(jax.random.fold_in(_rk, 8), (4,), 0, max(1, 512 // 4) + 1, jnp.int32)
        fside_BxS2xS2_0 = -3.05549e-07 + 0.0199987 * jax.random.normal(jax.random.fold_in(_rk, 11), (4, 512, 512), jnp.float32)
        _ctx_1024P = jax.random.normal(jax.random.fold_in(_rk, 12), (4, 16, 256), jnp.float32)
        _ctx_1024c = jax.random.dirichlet(jax.random.fold_in(_rk, 512), 0.3 * jnp.ones((16,), jnp.float32), (4, 512))
        _ctx_1024t = jnp.einsum('bsk,bkd->bsd', _ctx_1024c, _ctx_1024P)
        _ctx_1024t = _ctx_1024t * jax.lax.rsqrt(jnp.mean(jnp.square(_ctx_1024t)) + 1e-12) * 0.953939
        ctx_1024 = 6.82029e-06 + 0.0200006 * (_ctx_1024t + 0.3 * jax.random.normal(jax.random.fold_in(_rk, 612), (4, 512, 256), jnp.float32))
        return (x, fside_BxS2xS2_0, ctx_1024)
    x, fside_BxS2xS2_0, ctx_1024 = _rec_inputs()

    def _L0_xattn_setup():
        import jax, jax.numpy as jnp
        import numpy as np
        EPS = 1e-06
        QMAX = 127.0

        def _smooth_quant_linear(x, w):
            amax_x = jnp.max(jnp.abs(x), axis=0)
            amax_w = jnp.max(jnp.abs(w), axis=0)
            s = jnp.sqrt(jnp.maximum(amax_x, EPS) / jnp.maximum(amax_w, EPS))
            s = jnp.maximum(s, EPS)
            xs = x / s
            ws = w * s
            x_scale = jnp.maximum(jnp.max(jnp.abs(xs), axis=-1, keepdims=True), EPS) / QMAX
            w_scale = jnp.maximum(jnp.max(jnp.abs(ws), axis=-1, keepdims=True), EPS) / QMAX
            x_q = jnp.clip(jnp.round(xs / x_scale), -QMAX, QMAX)
            w_q = jnp.clip(jnp.round(ws / w_scale), -QMAX, QMAX)
            return x_q @ w_q.T * x_scale * w_scale.T

        def _expert_forward(xe, guw, dw):
            h = _smooth_quant_linear(xe, guw)
            gate, up = jnp.split(h, 2, axis=-1)
            a = jax.nn.silu(gate) * up
            return _smooth_quant_linear(a, dw)
        key = jax.random.key(seed)
        k1, k2, k3 = jax.random.split(key, 3)
        E, T, D, I = (8, 512, 512, 256)
        x = jax.random.normal(k1, (E, T, D), dtype=jnp.float32)
        gate_up_weight = jax.random.normal(k2, (E, 2 * I, D), dtype=jnp.float32) * 0.02
        down_weight = jax.random.normal(k3, (E, D, I), dtype=jnp.float32) * 0.02
        return {'x': x, 'gate_up_weight': gate_up_weight, 'down_weight': down_weight}
    _L0_xattn_all = _L0_xattn_setup()
    _L0_xattn_in = {k: v for k, v in _L0_xattn_all.items() if k in ()}
    del _L0_xattn_all

    def _L0_ffn_setup():
        import jax, jax.numpy as jnp
        import numpy as np
        B, S, D = (2, 1024, 512)
        E, DFF = (8, 2048)
        TOP_K = 2
        key = jax.random.key(seed)
        ks = jax.random.split(key, 4)
        scale_in = 1.0 / np.sqrt(D)
        scale_ff = 1.0 / np.sqrt(DFF)
        return {'hidden_states': jax.random.normal(ks[0], (B, S, D), dtype=jnp.float32), 'gate_w': jax.random.normal(ks[1], (E, D), dtype=jnp.float32) * scale_in, 'w1': jax.random.normal(ks[2], (E, D, DFF), dtype=jnp.float32) * scale_in, 'b1': jnp.zeros((E, DFF), dtype=jnp.float32), 'w2': jax.random.normal(ks[3], (E, DFF, D), dtype=jnp.float32) * scale_ff, 'b2': jnp.zeros((E, D), dtype=jnp.float32)}
    _L0_ffn_all = _L0_ffn_setup()
    _L0_ffn_in = {k: v for k, v in _L0_ffn_all.items() if k in ('gate_w', 'w1', 'b1', 'w2', 'b2')}
    del _L0_ffn_all
    return {'x': x, 'fside_BxS2xS2_0': fside_BxS2xS2_0, 'ctx_1024': ctx_1024, 'L0_ffn_gate_w': _L0_ffn_in['gate_w'], 'L0_ffn_w1': _L0_ffn_in['w1'], 'L0_ffn_b1': _L0_ffn_in['b1'], 'L0_ffn_w2': _L0_ffn_in['w2'], 'L0_ffn_b2': _L0_ffn_in['b2']}

def reference(x, fside_BxS2xS2_0, ctx_1024, L0_ffn_gate_w, L0_ffn_w1, L0_ffn_b1, L0_ffn_w2, L0_ffn_b2):
    import jax
    import jax.numpy as jnp

    def _L0_xattn_ref(x, gate_up_weight, down_weight):
        import jax, jax.numpy as jnp
        import numpy as np
        EPS = 1e-06
        QMAX = 127.0

        def _smooth_quant_linear(x, w):
            amax_x = jnp.max(jnp.abs(x), axis=0)
            amax_w = jnp.max(jnp.abs(w), axis=0)
            s = jnp.sqrt(jnp.maximum(amax_x, EPS) / jnp.maximum(amax_w, EPS))
            s = jnp.maximum(s, EPS)
            xs = x / s
            ws = w * s
            x_scale = jnp.maximum(jnp.max(jnp.abs(xs), axis=-1, keepdims=True), EPS) / QMAX
            w_scale = jnp.maximum(jnp.max(jnp.abs(ws), axis=-1, keepdims=True), EPS) / QMAX
            x_q = jnp.clip(jnp.round(xs / x_scale), -QMAX, QMAX)
            w_q = jnp.clip(jnp.round(ws / w_scale), -QMAX, QMAX)
            return x_q @ w_q.T * x_scale * w_scale.T

        def _expert_forward(xe, guw, dw):
            h = _smooth_quant_linear(xe, guw)
            gate, up = jnp.split(h, 2, axis=-1)
            a = jax.nn.silu(gate) * up
            return _smooth_quant_linear(a, dw)
        return jax.vmap(_expert_forward)(x, gate_up_weight, down_weight)

    def _L0_ffn_ref(hidden_states, gate_w, w1, b1, w2, b2):
        import jax, jax.numpy as jnp
        import numpy as np
        B, S, D = (2, 1024, 512)
        E, DFF = (8, 2048)
        TOP_K = 2
        b, s, d = hidden_states.shape
        x = hidden_states.reshape(-1, d)
        router_logits = x @ gate_w.T
        _, sel = jax.lax.top_k(router_logits.sum(axis=0), TOP_K)
        rw = jax.nn.softmax(router_logits[:, sel].astype(jnp.float32), axis=1)
        rw = rw.astype(x.dtype)
        w1s, b1s = (w1[sel], b1[sel])
        w2s, b2s = (w2[sel], b2[sel])
        h = jax.nn.gelu(jnp.einsum('nd,kdf->knf', x, w1s) + b1s[:, None, :])
        y = jnp.einsum('knf,kfd->knd', h, w2s) + b2s[:, None, :]
        out = jnp.einsum('nk,knd->nd', rw, y)
        return out.reshape(b, s, -1)
    x = x + _L0_xattn_ref(_layernorm(x, axis=-1), fside_BxS2xS2_0, ctx_1024)
    x = x + _L0_ffn_ref(_layernorm(x, axis=-1), L0_ffn_gate_w, L0_ffn_w1, L0_ffn_b1, L0_ffn_w2, L0_ffn_b2)
    return x

_drawn_inputs = setup_inputs


def setup_inputs(seed=0):
    import zlib

    import numpy as np

    out = dict(_drawn_inputs(seed))
    spreads = {'L0_ffn_b1': (0.0, 0.1), 'L0_ffn_b2': (0.0, 0.1)}
    factors = {}
    for name, (base, spread) in spreads.items():
        noise = np.random.default_rng([zlib.crc32(name.encode()), seed]).standard_normal(out[name].shape)
        drawn = base * np.exp(spread * noise) if base else spread * noise
        out[name] = jnp.asarray(drawn.astype(out[name].dtype))
    for name, factor in factors.items():
        out[name] = (out[name] * factor).astype(out[name].dtype)
    return out
```

```python
from contextlib import ExitStack

import concourse.bass as bass
from concourse import mybir

ALU = mybir.AluOpType
ACT = mybir.ActivationFunctionType
F32 = mybir.dt.float32
F32R = mybir.dt.float32r
BF16 = mybir.dt.bfloat16
U32 = mybir.dt.uint32
AX = mybir.AxisListType
ds = bass.ds

P = 128
QEPS = 1e-06
QMAX = 127.0
LN_EPS = 1e-05
ROUND = 12582912.0
EULER = 2.718281828459045


def xattn_ffn(
    nc: bass.Bass,
    x: bass.AP,
    gate_up: bass.AP,
    ctx_w: bass.AP,
    gate_w: bass.AP,
    w1: bass.AP,
    b1: bass.AP,
    w2: bass.AP,
    b2: bass.AP,
    out: bass.AP,
):
    B, T, D = x.shape
    O = gate_up.shape[1]
    I = ctx_w.shape[2]
    E, _, DFF = w1.shape
    TOPK = 2
    LANES = 2
    ROUNDS = B // LANES
    TT = T // P
    KD = D // P
    KI = I // P
    OT = O // P
    NT = B * TT
    FT = 4
    GROUPS = DFF // (FT * P)
    PAIRS = TOPK * GROUPS // 2
    assert O == 2 * I and T == 512 and D == 512 and OT == TT == KD == 4

    x_v = x.rearrange("b (p j) d -> b p j d", j=TT)
    out_v = out.rearrange("b (p j) d -> b p j d", j=TT)
    wt_v = gate_up.rearrange("b (j p) d -> b p j d", p=P)
    cx_v = ctx_w.rearrange("b (j p) i -> b p j i", p=P)
    w1_v = w1.rearrange("e (k p) (u f) -> e u p k f", p=P, f=P)
    w2_v = w2.rearrange("e (u f) d -> e u f d", f=P)
    b1_v = b1.rearrange("e (u f) -> e u f", f=P)

    with ExitStack() as ctx:
        def sb(name, shape, dt=F32, stack=ctx):
            return stack.enter_context(nc.sbuf_tensor(name, shape, dt))

        def sem(name):
            return ctx.enter_context(nc.semaphore(name))

        def lanes(name):
            return [sem(f"{name}{q}") for q in range(LANES)]

        bank = [ctx.enter_context(nc.psum_tensor(f"bank{i}", [P, 512], F32)) for i in range(8)]

        res = sb("res", [P, NT, D])
        xt_hi = sb("xt_hi", [P, KD, B * T], F32R)
        xt_lo = sb("xt_lo", [P, KD, B * T], F32R)
        ident = sb("ident", [P, P])
        ones = sb("ones", [P, P])
        iota8 = sb("iota8", [P, E])
        neg_half = sb("neg_half", [P, 4])
        half = sb("half", [P, 4])
        euler = sb("euler", [P, TOPK * NT])
        gw_rows = sb("gw_rows", [E, D])
        gwt_hi = sb("gwt_hi", [P, KD, E], F32R)
        gwt_lo = sb("gwt_lo", [P, KD, E], F32R)
        logits_t = sb("logits_t", [E, B * T])
        logit_part = sb("logit_part", [E, B])
        logit_sum = sb("logit_sum", [E, 1])
        sum_row = sb("sum_row", [P, E])
        top_v = sb("top_v", [P, 8])
        top_i = sb("top_i", [P, 8], U32)
        top_f = sb("top_f", [P, 8])
        onehot = sb("onehot", [P, TOPK, E])
        picked = sb("picked", [P, NT, E])
        lk = sb("lk", [P, TOPK, NT])
        lmax = sb("lmax", [P, NT])
        lsub = sb("lsub", [P, TOPK, NT])
        lexp = sb("lexp", [P, TOPK, NT])
        lden = sb("lden", [P, NT])
        lrec = sb("lrec", [P, NT])
        rw = sb("rw", [P, PAIRS, NT])
        b1_rows = sb("b1_rows", [TOPK * GROUPS * FT, P])
        b1_col = sb("b1_col", [P, TOPK * GROUPS * FT])

        early = ExitStack()

        def lane_sb(name, shape, dt=F32):
            return [sb(f"{name}{q}", shape, dt, early) for q in range(LANES)]

        wt = lane_sb("wt", [P, OT, D])
        cx = lane_sb("cx", [P, OT, I])
        xn = lane_sb("xn", [P, TT, D])
        xs = lane_sb("xs", [P, TT, D])
        ws = lane_sb("ws", [P, OT, D])
        xq = lane_sb("xq", [P, KD, T], BF16)
        wq = lane_sb("wq", [P, KD, O], BF16)
        av = lane_sb("av", [P, TT, I])
        wsc_row = lane_sb("wsc_row", [P, O])
        amax_x = lane_sb("amax_x", [P, D])
        amax_w = lane_sb("amax_w", [P, D])
        amax_c = lane_sb("amax_c", [P, I])
        stats = lane_sb("stats", [P, TT, 6])
        mv = lane_sb("mv", [P, TT, 2])
        var_e = lane_sb("var_e", [P, TT])
        rstd = lane_sb("rstd", [P, TT])
        nmr = lane_sb("nmr", [P, TT])
        cmax = lane_sb("cmax", [P, 2, KD])
        cmax_c = lane_sb("cmax_c", [P, KI])
        cclip = lane_sb("cclip", [P, 2, KD])
        crec = lane_sb("crec", [P, KD])
        ratio = lane_sb("ratio", [P, KD])
        sroot = lane_sb("sroot", [P, KD])
        smooth = lane_sb("smooth", [P, 2, KD])
        rmax = lane_sb("rmax", [P, 2, TT])
        scale = lane_sb("scale", [P, 2, TT])
        rscale = lane_sb("rscale", [P, 2, TT])
        early.close()

        raw1 = sb("raw1", [P, FT, KD, P])
        raw2 = sb("raw2", [P, FT, D])
        w1_hi = [sb(f"w1_hi{h}", [P, FT, KD, P], F32R) for h in range(2)]
        w1_lo = [sb(f"w1_lo{h}", [P, FT, KD, P], F32R) for h in range(2)]
        w2_hi = [sb(f"w2_hi{h}", [P, FT, D], F32R) for h in range(2)]
        w2_lo = [sb(f"w2_lo{h}", [P, FT, D], F32R) for h in range(2)]
        hid = [sb(f"hid{h}", [P, T]) for h in range(2)]
        h_hi = [sb(f"h_hi{h}", [P, T], F32R) for h in range(2)]
        h_lo = [sb(f"h_lo{h}", [P, T], F32R) for h in range(2)]
        b2_row = sb("b2_row", [P, TOPK, D])

        consts_ready = sem("consts_ready")
        own_wait = sem("own_wait")
        x_load = [sem(f"x_load{b}") for b in range(B)]
        wt_load = [sem(f"wt_load{b}") for b in range(B)]
        cx_load = [sem(f"cx_load{b}") for b in range(B)]
        gw_load = sem("gw_load")
        x_in, wt_in, cx_in = lanes("x_in"), lanes("wt_in"), lanes("cx_in")
        wt_used, cx_used = lanes("wt_used"), lanes("cx_used")
        dve_link = sem("dve_link")
        pool_link = sem("pool_link")
        gwt_ps, gwt_ready = sem("gwt_ps"), sem("gwt_ready")
        var_ready, rstd_ready, nmr_ready = lanes("var_ready"), lanes("rstd_ready"), lanes("nmr_ready")
        xn_ready = lanes("xn_ready")
        amaxw_ready, amaxx_ready = lanes("amaxw_ready"), lanes("amaxx_ready")
        amaxw_t, amaxx_t = lanes("amaxw_t"), lanes("amaxx_t")
        ratio_ready, root_ready, smooth_ready = lanes("ratio_ready"), lanes("root_ready"), lanes("smooth_ready")
        smooth_rows = lanes("smooth_rows")
        xscale_ready, wscale_ready = lanes("xscale_ready"), lanes("wscale_ready")
        xr_ready, wr_ready = lanes("xr_ready"), lanes("wr_ready")
        xt_ps, wt_ps = lanes("xt_ps"), lanes("wt_ps")
        xq_ready, wq_ready = lanes("xq_ready"), lanes("wq_ready")
        wrow_ps, wrow_ready = lanes("wrow_ps"), lanes("wrow_ready")
        prod_ready = lanes("prod_ready")
        gu_ready, silu_ready = lanes("gu_ready"), lanes("silu_ready")
        xn2t_ps, hi_ready, lo_ready = lanes("xn2t_ps"), lanes("hi_ready"), lanes("lo_ready")
        logit_ps, logit_ready = lanes("logit_ps"), lanes("logit_ready")
        sum_ready, sumrow_ps, top_ready = sem("sum_ready"), sem("sumrow_ps"), sem("top_ready")
        logcol_ps, lsub_ready, lexp_ready = sem("logcol_ps"), sem("lsub_ready"), sem("lexp_ready")
        raw1_load = [sem(f"raw1_load{s}") for s in range(FT)]
        raw2_load = [sem(f"raw2_load{s}") for s in range(FT)]
        b1_load, b2_load = sem("b1_load"), sem("b2_load")
        b1_ps, b1_ready = sem("b1_ps"), sem("b1_ready")
        raw_in = sem("raw_in")
        w_hi_ready, w_ready = sem("w_hi_ready"), sem("w_ready")
        up_ready, hid_ready, h_ready = sem("up_ready"), sem("hid_ready"), sem("h_ready")
        y_ready, y_free = sem("y_ready"), sem("y_free")
        stored = sem("stored")

        up_bank, y_bank = bank[0:2], bank[4:8]
        STEPS = FT * B
        block = ctx.enter_context(nc.Block())

        @block.sync
        def _(sp):
            sp.dma_start(gw_rows[:, :], gate_w).then_inc(gw_load, 16)
            for r in range(ROUNDS):
                for q in range(LANES):
                    b = r * LANES + q
                    sp.dma_start(res[:, b * TT:(b + 1) * TT, :], x_v[b]).then_inc(x_load[b], 16)
                    if r:
                        sp.wait_ge(wt_used[q], r)
                    sp.dma_start(wt[q][:, :, :], wt_v[b]).then_inc(wt_load[b], 16)
                    if r:
                        sp.wait_ge(cx_used[q], r)
                    sp.dma_start(cx[q][:, :, :], cx_v[b]).then_inc(cx_load[b], 16)
                for q in range(LANES):
                    b = r * LANES + q
                    sp.wait_ge(x_load[b], 16)
                    sp.sem_inc(x_in[q], 1)
                    sp.wait_ge(wt_load[b], 16)
                    sp.sem_inc(wt_in[q], 1)
                    sp.wait_ge(cx_load[b], 16)
                    sp.sem_inc(cx_in[q], 1)

            sp.wait_ge(top_ready, 1)
            expert = [sp.value_load(top_i[0:1, k:k + 1], min_val=0, max_val=E - 1) for k in range(TOPK)]

            def load_unit(e, u, s):
                sp.dma_start(raw1[:, s, :, :], w1_v[ds(e, 1), ds(u, 1)].rearrange("e u p k f -> (e u p) k f")
                             ).then_inc(raw1_load[s], 16)
                sp.dma_start(raw2[:, s, :], w2_v[ds(e, 1), ds(u, 1)].rearrange("e u f d -> (e u f) d")
                             ).then_inc(raw2_load[s], 16)

            for s in range(FT):
                load_unit(expert[0], s, s)
                if s == 0:
                    for k in range(TOPK):
                        sp.dma_start(b1_rows[k * GROUPS * FT:(k + 1) * GROUPS * FT, :],
                                     b1_v[ds(expert[k], 1)].rearrange("e u f -> (e u) f")).then_inc(b1_load, 16)
            for k in range(TOPK):
                sp.dma_start(b2_row[:, k, :], b2[ds(expert[k], 1), :].to_broadcast([P, D])).then_inc(b2_load, 16)
            for s in range(FT):
                sp.wait_ge(raw1_load[s], 16)
                sp.sem_inc(raw_in, 1)
                sp.wait_ge(raw2_load[s], 16)
                sp.sem_inc(raw_in, 1)
            for g in range(1, TOPK * GROUPS):
                for s in range(FT):
                    sp.wait_ge(w_ready, 2 * ((g - 1) * FT + s) + 2)
                    load_unit(expert[g // GROUPS], (g % GROUPS) * FT + s, s)
                    sp.wait_ge(raw1_load[s], 16 * (g + 1))
                    sp.sem_inc(raw_in, 1)
                    sp.wait_ge(raw2_load[s], 16 * (g + 1))
                    sp.sem_inc(raw_in, 1)
            before = TT + (TOPK * GROUPS - 1) * NT
            for b in range(B - 1):
                sp.wait_ge(y_free, before + (b + 1) * TT)
                sp.dma_start(out_v[b], res[:, b * TT:(b + 1) * TT, :]).then_inc(stored, 16)
            for j in range(TT):
                sp.wait_ge(y_free, before + (B - 1) * TT + j + 1)
                sp.dma_start(out_v[B - 1, :, j, :], res[:, (B - 1) * TT + j, :]).then_inc(stored, 16)
            sp.wait_ge(stored, 16 * (B - 1 + TT))

        @block.gpsimd
        def _(pool):
            g = nc.gpsimd
            g.memset(ident[:, :], 0.0).then_inc(pool_link, 1)
            g.memset(ones[:, :], 1.0)
            g.memset(half[:, :], 0.5)
            g.memset(neg_half[:, :], -0.5)
            g.memset(euler[:, :], EULER)
            g.iota(iota8[:, :], pattern=[[1, E]], base=0, channel_multiplier=0,
                   allow_small_or_imprecise_dtypes=True)
            pool.wait_ge(pool_link, 1)
            g.affine_select(out=ident[:, :], in_=ident[:, :], compare_op=ALU.not_equal, fill=1.0, base=0,
                            pattern=[[-1, P]], channel_multiplier=1).then_inc(consts_ready, 1)

            def root(q, i, c, n):
                pool.wait_ge(ratio_ready[q], 2 * i + c)
                g.tensor_tensor(sroot[q][:, 0:n], ratio[q][:, 0:n], half[:, 0:n], ALU.pow).then_inc(root_ready[q], 1)

            def round_weight(q, i, c, n):
                pool.wait_ge(wscale_ready[q], 2 * i + c)
                pool.sem_inc(own_wait, 1)
                for j in range(OT):
                    v = ws[q][:, j, 0:n]
                    g.tensor_scalar(v, v, rscale[q][:, 1, j:j + 1], ROUND, ALU.mult, ALU.add
                                    ).then_inc(wr_ready[q], 1)

            def inv_std(q, i, c):
                pool.wait_ge(var_ready[q], 2 * i + c)
                g.tensor_tensor(rstd[q][:, :], var_e[q][:, :], neg_half[:, :], ALU.pow).then_inc(rstd_ready[q], 1)

            with pool.Fori(0, ROUNDS) as i:
                for q in range(LANES):
                    inv_std(q, i, 1)
                for q in range(LANES):
                    root(q, i, 1, KD)
                for q in range(LANES):
                    round_weight(q, i, 1, D)
                for q in range(LANES):
                    root(q, i, 2, KI)
                for q in range(LANES):
                    round_weight(q, i, 2, I)
                for q in range(LANES):
                    inv_std(q, i, 2)
            pool.wait_ge(lsub_ready, TOPK)
            g.tensor_tensor(lexp[:, :, :].rearrange("p k n -> p (k n)"), euler[:, :],
                            lsub[:, :, :].rearrange("p k n -> p (k n)"), ALU.pow).then_inc(lexp_ready, 1)

        @block.tensor
        def _(pe):
            t = nc.tensor

            def bk(q, k):
                return bank[4 * q + k]

            pe.wait_ge(consts_ready, 1)
            pe.wait_ge(gw_load, 16)
            for k in range(KD):
                last = t.transpose(bank[0][:, k * E:(k + 1) * E], gw_rows[:, k * P:(k + 1) * P], ident[0:E, 0:E])
            last.then_inc(gwt_ps, 1)

            def transpose_wmax(q, i):
                pe.wait_ge(amaxw_ready[q], i + 1)
                if q == 0:
                    pe.wait_ge(gwt_ready, 1)
                for k in range(KI):
                    t.transpose(bk(q, 1)[:, k * P:(k + 1) * P], amax_c[q][:, k * P:(k + 1) * P], ident[:, :])
                for k in range(KD):
                    last = t.transpose(bk(q, 0)[:, k * P:(k + 1) * P], amax_w[q][:, k * P:(k + 1) * P], ident[:, :])
                last.then_inc(amaxw_t[q], 1)

            def transpose_xmax(q, i, c, n, to):
                pe.wait_ge(amaxx_ready[q], 2 * i + c)
                for k in range(n):
                    last = t.transpose(bk(q, to)[:, k * P:(k + 1) * P], amax_x[q][:, k * P:(k + 1) * P], ident[:, :])
                last.then_inc(amaxx_t[q], 1)

            def spread(dst, col):
                return t.matmul(dst, col.to_broadcast([P, P]), ident[:, :], start=True, stop=True)

            def smooth_to_rows(q, i, c, n, to):
                pe.wait_ge(smooth_ready[q], 2 * i + c)
                for w in range(2):
                    b, o = to[w]
                    for k in range(n):
                        last = spread(bk(q, b)[:, o + k * P:o + (k + 1) * P], smooth[q][:, w, k:k + 1])
                last.then_inc(smooth_rows[q], 1)

            def transpose_x(q, i, c, n, to):
                base = i * (KD + KI) + (c - 1) * KD
                for k in range(n):
                    for j in range(TT):
                        if k == 0:
                            pe.wait_ge(xr_ready[q], 2 * TT * i + TT * (c - 1) + j + 1)
                        last = t.transpose(bk(q, to[k])[:, j * P:(j + 1) * P], xs[q][:, j, k * P:(k + 1) * P],
                                           ident[:, :])
                    last.then_inc(xt_ps[q], 1)
                return base

            def transpose_w(q, i, c, n, to, free):
                for k in range(n):
                    if free is not None:
                        free(k)
                    for j in range(OT):
                        if k == 0:
                            pe.wait_ge(wr_ready[q], 2 * OT * i + OT * (c - 1) + j + 1)
                        last = t.transpose(bk(q, to[k])[:, j * P:(j + 1) * P], ws[q][:, j, k * P:(k + 1) * P],
                                           ident[:, :])
                    last.then_inc(wt_ps[q], 1)

            def scales_to_row(q, i, c, to):
                pe.wait_ge(wscale_ready[q], 2 * i + c)
                for j in range(OT):
                    last = spread(bk(q, to)[:, j * P:(j + 1) * P], scale[q][:, 1, j:j + 1])
                last.then_inc(wrow_ps[q], 1)

            NQ = KD + KI

            def product(q, i, c, n):
                done = NQ * i + (KD if c == 1 else NQ)
                pe.wait_ge(xq_ready[q], done)
                pe.wait_ge(wq_ready[q], done)
                pe.wait_ge(wrow_ready[q], 2 * i + c)
                for j in range(TT):
                    for k in range(n):
                        last = t.matmul(bk(q, j)[:, 0:O], xq[q][:, k, j * P:(j + 1) * P], wq[q][:, k, :],
                                        start=(k == 0), stop=(k == n - 1))
                    last.then_inc(prod_ready[q], 1)

            def transpose_xn2(q, i):
                for k in range(KD):
                    for j in range(TT):
                        if k == 0:
                            pe.wait_ge(xn_ready[q], 2 * TT * i + TT + j + 1)
                        last = t.transpose(bk(q, k)[:, j * P:(j + 1) * P], xn[q][:, j, k * P:(k + 1) * P],
                                           ident[:, :])
                    last.then_inc(xn2t_ps[q], 1)

            def router(q, i):
                pe.wait_ge(lo_ready[q], KD * i + KD)
                at = (LANES * i + q) * T
                n = 0
                for k in range(KD):
                    for a, v in ((gwt_hi, xt_hi), (gwt_hi, xt_lo), (gwt_lo, xt_hi)):
                        last = t.matmul(bk(q, 3)[0:E, :], a[:, k, :], v[:, k, ds(at, T)],
                                        start=(n == 0), stop=(n == 3 * KD - 1))
                        n += 1
                last.then_inc(logit_ps[q], 1)

            with pe.Fori(0, ROUNDS) as i:
                for q in range(LANES):
                    transpose_wmax(q, i)
                for q in range(LANES):
                    transpose_xmax(q, i, 1, KD, 2)
                for q in range(LANES):
                    smooth_to_rows(q, i, 1, KD, ((2, 0), (3, 0)))
                for q in range(LANES):
                    transpose_x(q, i, 1, KD, (0, 1, 2, 3))
                for q in range(LANES):
                    pe.wait_ge(xq_ready[q], NQ * i + 1)
                    scales_to_row(q, i, 1, 0)

                    def free(k, q=q):
                        if k < KD - 1:
                            pe.wait_ge(xq_ready[q], NQ * i + k + 2)
                        else:
                            pe.wait_ge(wrow_ready[q], 2 * i + 1)
                    transpose_w(q, i, 1, KD, (1, 2, 3, 0), free)
                for q in range(LANES):
                    product(q, i, 1, KD)
                for q in range(LANES):
                    transpose_xmax(q, i, 2, KI, 0)
                for q in range(LANES):
                    smooth_to_rows(q, i, 2, KI, ((1, 0), (1, I)))
                for q in range(LANES):
                    transpose_x(q, i, 2, KI, (2, 3))
                for q in range(LANES):
                    transpose_w(q, i, 2, KI, (0, 1), None)
                    pe.wait_ge(xq_ready[q], NQ * i + KD + 1)
                    scales_to_row(q, i, 2, 2)
                for q in range(LANES):
                    product(q, i, 2, KI)
                for q in range(LANES):
                    transpose_xn2(q, i)
                for q in range(LANES):
                    router(q, i)

            pe.wait_ge(sum_ready, 1)
            t.matmul(bank[1][:, 0:E], logit_sum[:, 0:1].to_broadcast([E, P]), ident[0:E, 0:E],
                     start=True, stop=True).then_inc(sumrow_ps, 1)
            for n in range(NT):
                last = t.transpose(bank[3][:, n * E:(n + 1) * E], logits_t[:, n * P:(n + 1) * P], ident[0:E, 0:E])
            last.then_inc(logcol_ps, 1)
            pe.wait_ge(b1_load, 16 * TOPK)
            t.transpose(bank[2][:, 0:TOPK * GROUPS * FT], b1_rows[:, :],
                        ident[0:TOPK * GROUPS * FT, 0:TOPK * GROUPS * FT]).then_inc(b1_ps, 1)

            def up(group, h, f, at):
                pe.wait_ge(w_ready, 2 * (group * FT + f) + 1)
                n = 0
                for k in range(KD):
                    for a, v in ((w1_hi, xt_hi), (w1_hi, xt_lo), (w1_lo, xt_hi)):
                        last = t.matmul(up_bank[f % 2][:, :], a[h][:, f, k, :], v[:, k, ds(at, T)],
                                        start=(n == 0), stop=(n == 3 * KD - 1))
                        n += 1
                last.then_inc(up_ready, 1)

            def down(group, h, f, b):
                pe.wait_ge(w_ready, 2 * (group * FT + f) + 2)
                pe.wait_ge(h_ready, group * STEPS + b * FT + f + 1)
                for j in range(TT):
                    if f == 0:
                        pe.wait_ge(y_free, group * NT + b * TT + j + 1)
                    n = 0
                    for a, v in ((h_hi, w2_hi), (h_hi, w2_lo), (h_lo, w2_hi)):
                        last = t.matmul(y_bank[j][:, :], a[f % 2][:, j * P:(j + 1) * P], v[h][:, f, :],
                                        start=(f == 0 and n == 0), stop=(f == FT - 1 and n == 2),
                                        skip_group_check=True)
                        n += 1
                    if f == FT - 1:
                        last.then_inc(y_ready, 1)

            def pair_of_groups(p, final):
                for h in range(2):
                    group = 2 * p + h
                    with pe.Fori(0, B - 1) as b:
                        for f in range(FT):
                            if f < FT - 1:
                                up(group, h, f + 1, b * T)
                            else:
                                up(group, h, 0, b * T + T)
                            down(group, h, f, b)
                    for f in range(FT):
                        if f < FT - 1:
                            up(group, h, f + 1, (B - 1) * T)
                        elif not (final and h):
                            up(group + 1, 1 - h, 0, 0)
                        down(group, h, f, B - 1)

            up(0, 0, 0, 0)
            with pe.Fori(0, PAIRS - 1) as p:
                pair_of_groups(p, False)
            pair_of_groups(PAIRS - 1, True)

        @block.scalar
        def _(act):
            s = nc.scalar

            def bk(q, k):
                return bank[4 * q + k]

            def normalise(q, i, c):
                act.wait_ge(nmr_ready[q], 2 * i + c)
                act.sem_inc(own_wait, 1)
                b = LANES * i + q
                for j in range(TT):
                    s.activation(xn[q][:, j, :], res[:, ds(b * TT + j, 1), :].rearrange("p o d -> p (o d)"),
                                 ACT.Identity, bias=nmr[q][:, j:j + 1], scale=rstd[q][:, j:j + 1]
                                 ).then_inc(xn_ready[q], 1)

            def round_x(q, i, c, n):
                act.wait_ge(xscale_ready[q], 2 * i + c)
                for j in range(TT):
                    v = xs[q][:, j, 0:n]
                    s.activation(v, v, ACT.Copy, bias=ROUND, scale=rscale[q][:, 0, j:j + 1]
                                 ).then_inc(xr_ready[q], 1)

            NQ = KD + KI

            def integers_x(q, i, c, n, frm):
                for k in range(n):
                    act.wait_ge(xt_ps[q], NQ * i + (c - 1) * KD + k + 1)
                    s.activation(xq[q][:, k, :], bk(q, frm[k])[:, :], ACT.Copy, bias=-ROUND).then_inc(xq_ready[q], 1)

            def keep_scale_row(q, i, c, frm):
                act.wait_ge(wrow_ps[q], 2 * i + c)
                s.copy(wsc_row[q][:, :], bk(q, frm)[:, :]).then_inc(wrow_ready[q], 1)

            with act.Fori(0, ROUNDS) as i:
                for q in range(LANES):
                    normalise(q, i, 1)
                for q in range(LANES):
                    round_x(q, i, 1, D)
                for q in range(LANES):
                    integers_x(q, i, 1, KD, (0, 1, 2, 3))
                    keep_scale_row(q, i, 1, 0)
                for q in range(LANES):
                    act.wait_ge(gu_ready[q], TT * i + TT)
                    s.activation(av[q][:, :, :], xn[q][:, :, 0:I], ACT.Silu).then_inc(silu_ready[q], 1)
                for q in range(LANES):
                    round_x(q, i, 2, I)
                for q in range(LANES):
                    integers_x(q, i, 2, KI, (2, 3))
                    keep_scale_row(q, i, 2, 2)
                for q in range(LANES):
                    normalise(q, i, 2)
                for q in range(LANES):
                    at = (LANES * i + q) * T
                    for k in range(KD):
                        act.wait_ge(xn2t_ps[q], KD * i + k + 1)
                        s.copy(xt_hi[:, k, ds(at, T)], bk(q, k)[:, :]).then_inc(hi_ready[q], 1)
                for q in range(LANES):
                    act.wait_ge(logit_ps[q], i + 1)
                    b = LANES * i + q
                    s.activation(logits_t[:, ds(b * T, T)], bk(q, 3)[0:E, :], ACT.Copy,
                                 accum_out=logit_part[:, ds(b, 1)]).then_inc(logit_ready[q], 1)

            def split_hi(n, w1_at, w2_at):
                act.wait_ge(raw_in, 2 * n + 1)
                s.copy(w1_at[1], w1_at[0]).then_inc(w_hi_ready, 1)
                act.wait_ge(raw_in, 2 * n + 2)
                s.copy(w2_at[1], w2_at[0]).then_inc(w_hi_ready, 1)

            for f in range(FT):
                split_hi(f, (raw1[:, f], w1_hi[0][:, f]), (raw2[:, f], w2_hi[0][:, f]))
                if f == 0:
                    act.wait_ge(b1_ps, 1)
                    s.copy(b1_col[:, :], bank[2][:, 0:TOPK * GROUPS * FT]).then_inc(b1_ready, 1)
                    act.wait_ge(b1_ready, 1)

            def pair_of_groups(p, final):
                for h in range(2):
                    group = 2 * p + h
                    with act.Fori(0, B) as b:
                        for f in range(FT):
                            act.wait_ge(up_ready, group * STEPS + b * FT + f + 1)
                            col = group * FT + f
                            bias = b1_col[:, ds(col, 1)]
                            s.activation(hid[f % 2][:, :], up_bank[f % 2][:, :], ACT.Gelu_apprx_tanh,
                                         bias=bias).then_inc(hid_ready, 1)
                            s.activation(h_hi[f % 2][:, :], up_bank[f % 2][:, :], ACT.Gelu_apprx_tanh,
                                         bias=bias).then_inc(hid_ready, 1)
                            nxt = 1 - h
                            if f == 2 and not (final and h):
                                n = (group + 1) * FT + b
                                act.wait_ge(raw_in, 2 * n + 2)
                                s.copy(w1_hi[nxt][:, ds(b, 1)], raw1[:, ds(b, 1)]).then_inc(w_hi_ready, 1)
                                s.copy(w2_hi[nxt][:, ds(b, 1)], raw2[:, ds(b, 1)]).then_inc(w_hi_ready, 1)

            with act.Fori(0, PAIRS - 1) as p:
                pair_of_groups(p, False)
            pair_of_groups(PAIRS - 1, True)

        @block.vector
        def _(dve):
            v = nc.vector

            def bk(q, k):
                return bank[4 * q + k]

            chain = [0, 0]

            def link(ins):
                chain[0] += 1
                ins.then_inc(dve_link, 1)
                dve.wait_ge(dve_link, chain[1] + chain[0])

            dve.wait_ge(gwt_ps, 1)
            g_ps = bank[0][:, 0:KD * E].rearrange("p (k e) -> p k e", e=E)
            link(v.tensor_copy(gwt_hi[:, :, :], g_ps))
            v.tensor_tensor(gwt_lo[:, :, :], g_ps, gwt_hi[:, :, :].bitcast(F32), ALU.subtract).then_inc(gwt_ready, 1)

            def moments(q, i, c):
                b = LANES * i + q
                dve.sem_inc(own_wait, 1)
                for j in range(TT):
                    ins = v.bn_stats(stats[q][:, j, :], res[:, ds(b * TT + j, 1), :].rearrange("p o d -> p (o d)"))
                link(ins)
                dve.sem_inc(own_wait, 1)
                for j in range(TT):
                    ins = v.bn_aggr(mv[q][:, j, :], stats[q][:, j, :])
                link(ins)
                v.tensor_scalar(var_e[q][:, :], mv[q][:, :, 1], LN_EPS, None, ALU.add).then_inc(var_ready[q], 1)

            def neg_mean(q, i, c):
                dve.wait_ge(rstd_ready[q], 2 * i + c)
                v.scalar_tensor_tensor(out=nmr[q][:, :], in0=mv[q][:, :, 0], scalar=-1.0, in1=rstd[q][:, :],
                                       op0=ALU.mult, op1=ALU.mult).then_inc(nmr_ready[q], 1)

            def abs_max(dst, src, eng_axis=AX.X):
                return v.tensor_reduce(dst, src, eng_axis, ALU.max, apply_absolute_value=True)

            def smoothing(q, i, c, n, act_bank):
                dve.wait_ge(amaxx_t[q], 2 * i + c)
                link(v.tensor_reduce(cmax[q][:, 0, 0:n],
                                     bk(q, act_bank)[:, 0:n * P].rearrange("p (k t) -> p k t", t=P), AX.X, ALU.max))
                link(v.tensor_scalar(cclip[q][:, :, 0:n], cmax[q][:, :, 0:n], QEPS, None, ALU.max))
                link(v.reciprocal(crec[q][:, 0:n], cclip[q][:, 1, 0:n]))
                v.tensor_tensor(ratio[q][:, 0:n], cclip[q][:, 0, 0:n], crec[q][:, 0:n], ALU.mult
                                ).then_inc(ratio_ready[q], 1)

            def inverse(q, i, c, n):
                dve.wait_ge(root_ready[q], 2 * i + c)
                link(v.tensor_scalar(smooth[q][:, 1, 0:n], sroot[q][:, 0:n], QEPS, None, ALU.max))
                v.reciprocal(smooth[q][:, 0, 0:n], smooth[q][:, 1, 0:n]).then_inc(smooth_ready[q], 1)

            def scaled(q, i, c, n, src_x, src_w, rows, used):
                dve.wait_ge(smooth_rows[q], 2 * i + c)
                row = [bk(q, b)[:, o:o + n].rearrange("p (o n) -> p o n", o=1).to_broadcast([P, TT, n])
                       for b, o in rows]
                v.tensor_tensor(xs[q][:, :, 0:n], src_x, row[0], ALU.mult).then_inc(dve_link, 1)
                v.tensor_tensor(ws[q][:, :, 0:n], src_w, row[1], ALU.mult).then_inc(dve_link, 1)
                chain[0] += 2
                dve.wait_ge(dve_link, chain[1] + chain[0])
                dve.sem_inc(used[q], 1)
                for w, (m, ready) in enumerate(((xs, xscale_ready), (ws, wscale_ready))):
                    link(abs_max(rmax[q][:, w, :], m[q][:, :, 0:n]))
                    link(v.tensor_scalar(scale[q][:, w, :], rmax[q][:, w, :], QEPS, 1.0 / QMAX, ALU.max, ALU.mult))
                    v.reciprocal(rscale[q][:, w, :], scale[q][:, w, :]).then_inc(ready[q], 1)

            NQ = KD + KI

            def integers_w(q, i, c, n, frm):
                for k in range(n):
                    dve.wait_ge(wt_ps[q], NQ * i + (c - 1) * KD + k + 1)
                    v.tensor_scalar(wq[q][:, k, :], bk(q, frm[k])[:, :], -ROUND, None, ALU.add
                                    ).then_inc(wq_ready[q], 1)

            def dequant(q, i, c, dst, ready):
                dve.wait_ge(wrow_ready[q], 2 * i + c)
                for j in range(TT):
                    dve.wait_ge(prod_ready[q], 2 * TT * i + TT * (c - 1) + j + 1)
                    ins = v.scalar_tensor_tensor(out=dst[:, j, :], in0=bk(q, j)[:, :],
                                                 scalar=scale[q][:, 0, j:j + 1], in1=wsc_row[q][:, :],
                                                 op0=ALU.mult, op1=ALU.mult)
                    ins.then_inc(ready, 1)

            with dve.Fori(0, ROUNDS) as i:
                chain[:] = [0, LINKS * i + 1]
                for q in range(LANES):
                    dve.wait_ge(x_in[q], i + 1)
                    moments(q, i, 1)
                for q in range(LANES):
                    dve.wait_ge(wt_in[q], i + 1)
                    v.tensor_reduce(amax_w[q][:, :], wt[q][:, :, :].rearrange("p j d -> p d j"), AX.X, ALU.max,
                                    apply_absolute_value=True)
                    dve.wait_ge(cx_in[q], i + 1)
                    v.tensor_reduce(amax_c[q][:, :], cx[q][:, :, :].rearrange("p j d -> p d j"), AX.X, ALU.max,
                                    apply_absolute_value=True).then_inc(amaxw_ready[q], 1)
                    neg_mean(q, i, 1)
                for q in range(LANES):
                    dve.wait_ge(amaxw_t[q], i + 1)
                    v.tensor_reduce(cmax[q][:, 1, :], bk(q, 0)[:, :].rearrange("p (k t) -> p k t", t=P),
                                    AX.X, ALU.max)
                    v.tensor_reduce(cmax_c[q][:, :], bk(q, 1)[:, 0:I].rearrange("p (k t) -> p k t", t=P),
                                    AX.X, ALU.max)
                    dve.wait_ge(xn_ready[q], 2 * TT * i + TT)
                    v.tensor_reduce(amax_x[q][:, :], xn[q][:, :, :].rearrange("p j d -> p d j"), AX.X, ALU.max,
                                    apply_absolute_value=True).then_inc(amaxx_ready[q], 1)
                for q in range(LANES):
                    smoothing(q, i, 1, KD, 2)
                for q in range(LANES):
                    inverse(q, i, 1, KD)
                for q in range(LANES):
                    scaled(q, i, 1, D, xn[q][:, :, :], wt[q][:, :, :], ((2, 0), (3, 0)), wt_used)
                for q in range(LANES):
                    integers_w(q, i, 1, KD, (1, 2, 3, 0))
                for q in range(LANES):
                    dequant(q, i, 1, xn[q], gu_ready[q])
                for q in range(LANES):
                    dve.wait_ge(silu_ready[q], i + 1)
                    link(v.tensor_tensor(av[q][:, :, :], av[q][:, :, :], xn[q][:, :, I:O], ALU.mult))
                    v.tensor_copy(cmax[q][:, 1, 0:KI], cmax_c[q][:, :])
                    v.tensor_reduce(amax_x[q][:, 0:I], av[q][:, :, :].rearrange("p j d -> p d j"), AX.X, ALU.max,
                                    apply_absolute_value=True).then_inc(amaxx_ready[q], 1)
                for q in range(LANES):
                    smoothing(q, i, 2, KI, 0)
                for q in range(LANES):
                    inverse(q, i, 2, KI)
                for q in range(LANES):
                    scaled(q, i, 2, I, av[q][:, :, :], cx[q][:, :, :], ((1, 0), (1, I)), cx_used)
                for q in range(LANES):
                    integers_w(q, i, 2, KI, (0, 1))
                for q in range(LANES):
                    dequant(q, i, 2, xs[q], dve_link)
                    chain[0] += TT
                    dve.wait_ge(dve_link, chain[1] + chain[0])
                    r = res[:, ds((LANES * i + q) * TT, TT), :]
                    link(v.tensor_tensor(r, r, xs[q][:, :, :], ALU.add))
                    moments(q, i, 2)
                for q in range(LANES):
                    neg_mean(q, i, 2)
                for q in range(LANES):
                    at = (LANES * i + q) * T
                    for k in range(KD):
                        dve.wait_ge(hi_ready[q], KD * i + k + 1)
                        v.tensor_tensor(xt_lo[:, k, ds(at, T)], bk(q, k)[:, :],
                                        xt_hi[:, k, ds(at, T)].bitcast(F32), ALU.subtract
                                        ).then_inc(lo_ready[q], 1)
                assert chain[0] == LINKS, chain[0]
            chain[:] = [0, LINKS * ROUNDS + 1]

            for q in range(LANES):
                dve.wait_ge(logit_ready[q], ROUNDS)
            v.tensor_reduce(logit_sum[:, :], logit_part[:, :], AX.X, ALU.add).then_inc(sum_ready, 1)
            dve.wait_ge(sumrow_ps, 1)
            link(v.tensor_copy(sum_row[:, :], bank[1][:, 0:E]))
            link(v.max(top_v[:, :], sum_row[:, :]))
            v.max_index(top_i[:, :], top_v[:, :], sum_row[:, :]).then_inc(top_ready, 1)
            dve.wait_ge(top_ready, 1)

            def split_lo(n, w1_at, w2_at):
                dve.wait_ge(w_hi_ready, 2 * n + 1)
                v.tensor_tensor(w1_at[2], w1_at[0], w1_at[1].bitcast(F32), ALU.subtract).then_inc(w_ready, 1)
                dve.wait_ge(w_hi_ready, 2 * n + 2)
                v.tensor_tensor(w2_at[2], w2_at[0], w2_at[1].bitcast(F32), ALU.subtract).then_inc(w_ready, 1)

            for f in range(FT):
                split_lo(f, (raw1[:, f], w1_hi[0][:, f], w1_lo[0][:, f]), (raw2[:, f], w2_hi[0][:, f], w2_lo[0][:, f]))
                if f == 0:
                    link(v.tensor_copy(top_f[:, :], top_i[:, :]))
                    for k in range(TOPK):
                        link(v.tensor_scalar(onehot[:, k, :], iota8[:, :], top_f[:, k:k + 1], None, ALU.is_equal))
                    dve.wait_ge(logcol_ps, 1)
                    cols = bank[3][:, 0:NT * E].rearrange("p (n e) -> p n e", e=E)
                    for k in range(TOPK):
                        link(v.tensor_tensor(picked[:, :, :], cols,
                                             onehot[:, k:k + 1, :].to_broadcast([P, NT, E]), ALU.mult))
                        link(v.tensor_reduce(lk[:, k, :], picked[:, :, :], AX.X, ALU.add))
                    link(v.tensor_tensor(lmax[:, :], lk[:, 0, :], lk[:, 1, :], ALU.max))
                    for k in range(TOPK):
                        v.tensor_tensor(lsub[:, k, :], lk[:, k, :], lmax[:, :], ALU.subtract).then_inc(lsub_ready, 1)
            dve.wait_ge(lexp_ready, 1)
            link(v.tensor_tensor(lden[:, :], lexp[:, 0, :], lexp[:, 1, :], ALU.add))
            link(v.reciprocal(lrec[:, :], lden[:, :]))
            for p in range(PAIRS):
                ins = v.tensor_tensor(rw[:, p, :], lexp[:, p * TOPK // PAIRS, :], lrec[:, :], ALU.mult)
            link(ins)
            dve.sem_inc(y_free, TT)

            def pair_of_groups(p, final):
                for h in range(2):
                    group = 2 * p + h
                    last_group = final and h == 1
                    with dve.Fori(0, B) as b:
                        for f in range(FT):
                            step = group * STEPS + b * FT + f
                            dve.wait_ge(hid_ready, 2 * step + 2)
                            v.tensor_tensor(h_lo[f % 2][:, :], hid[f % 2][:, :], h_hi[f % 2][:, :].bitcast(F32),
                                            ALU.subtract).then_inc(h_ready, 1)
                            nxt = 1 - h
                            if f == 2 and not last_group:
                                n = (group + 1) * FT + b
                                dve.wait_ge(w_hi_ready, 2 * n + 2)
                                v.tensor_tensor(w1_lo[nxt][:, ds(b, 1)], raw1[:, ds(b, 1)],
                                                w1_hi[nxt][:, ds(b, 1)].bitcast(F32), ALU.subtract
                                                ).then_inc(w_ready, 1)
                                v.tensor_tensor(w2_lo[nxt][:, ds(b, 1)], raw2[:, ds(b, 1)],
                                                w2_hi[nxt][:, ds(b, 1)].bitcast(F32), ALU.subtract
                                                ).then_inc(w_ready, 1)
                            if last_group and f < TOPK:
                                for j in range(TT):
                                    k = f
                                    r = res[:, ds(b * TT + j, 1), :].rearrange("p o d -> p (o d)")
                                    ins = v.scalar_tensor_tensor(
                                        out=r, in0=b2_row[:, k, :], scalar=rw[:, k * (PAIRS // TOPK), ds(b * TT + j, 1)],
                                        in1=r, op0=ALU.mult, op1=ALU.add)
                                ins.then_inc(dve_link, 1)
                                dve.wait_ge(dve_link, chain[1] + chain[0] + TOPK * b + f + 1)
                        for j in range(TT):
                            dve.wait_ge(y_ready, group * NT + b * TT + j + 1)
                            r = res[:, ds(b * TT + j, 1), :].rearrange("p o d -> p (o d)")
                            ins = v.scalar_tensor_tensor(
                                out=r, in0=y_bank[j][:, :], scalar=rw[:, p, ds(b * TT + j, 1)] if final else
                                rw[:, ds(p, 1), ds(b * TT + j, 1)].rearrange("p a b -> p (a b)"),
                                in1=r, op0=ALU.mult, op1=ALU.add)
                            ins.then_inc(y_free, 1)

            dve.wait_ge(b2_load, 16 * TOPK)
            with dve.Fori(0, PAIRS - 1) as p:
                pair_of_groups(p, False)
            pair_of_groups(PAIRS - 1, True)


LINKS = 60

_INS = ["x", "fside_BxS2xS2_0", "ctx_1024", "L0_ffn_gate_w", "L0_ffn_w1", "L0_ffn_b1", "L0_ffn_w2", "L0_ffn_b2"]
_OUT = (4, 512, 512)


def kernel(**inputs):
    import numpy as np
    import concourse.bacc as bacc
    from concourse.bass_utils import run_bass_kernel_spmd

    nc = bacc.Bacc("TRN2", target_bir_lowering=False, num_devices=1, dynamic_dma_scratch_size=1024)
    arrays, args = {}, []
    for name in _INS:
        a = np.ascontiguousarray(inputs[name])
        arrays[f"in_{name}"] = a
        args.append(nc.dram_tensor(f"in_{name}", a.shape, mybir.dt.from_np(a.dtype), kind="ExternalInput").ap())
    args.append(nc.dram_tensor("out_x", _OUT, F32, kind="ExternalOutput").ap())
    xattn_ffn(nc, *args)
    r = run_bass_kernel_spmd(nc, [arrays], core_ids=[0])
    return r.results[0]["out_x"]
```

```python
from contextlib import ExitStack

import concourse.bass as bass
from concourse import mybir

ALU = mybir.AluOpType
ACT = mybir.ActivationFunctionType
F32 = mybir.dt.float32
F32R = mybir.dt.float32r
BF16 = mybir.dt.bfloat16
U32 = mybir.dt.uint32
AX = mybir.AxisListType
ds = bass.ds

P = 128
QEPS = 1e-06
QMAX = 127.0
LN_EPS = 1e-05
ROUND = 12582912.0
EULER = 2.718281828459045


def xattn_ffn(
    nc: bass.Bass,
    x: bass.AP,
    gate_up: bass.AP,
    ctx_w: bass.AP,
    gate_w: bass.AP,
    w1: bass.AP,
    b1: bass.AP,
    w2: bass.AP,
    b2: bass.AP,
    out: bass.AP,
):
    B, T, D = x.shape
    O = gate_up.shape[1]
    I = ctx_w.shape[2]
    E, _, DFF = w1.shape
    TOPK = 2
    LANES = 2
    ROUNDS = B // LANES
    TT = T // P
    KD = D // P
    KI = I // P
    OT = O // P
    NT = B * TT
    FT = 4
    GROUPS = DFF // (FT * P)
    PAIRS = TOPK * GROUPS // 2
    assert O == 2 * I and T == 512 and D == 512 and OT == TT == KD == 4

    x_v = x.rearrange("b (p j) d -> b p j d", j=TT)
    out_v = out.rearrange("b (p j) d -> b p j d", j=TT)
    wt_v = gate_up.rearrange("b (j p) d -> b p j d", p=P)
    cx_v = ctx_w.rearrange("b (j p) i -> b p j i", p=P)
    w1_v = w1.rearrange("e (k p) (u f) -> e u p k f", p=P, f=P)
    w2_v = w2.rearrange("e (u f) d -> e u f d", f=P)
    b1_v = b1.rearrange("e (u f) -> e u f", f=P)

    with ExitStack() as ctx:
        def sb(name, shape, dt=F32, stack=ctx):
            return stack.enter_context(nc.sbuf_tensor(name, shape, dt))

        def sem(name):
            return ctx.enter_context(nc.semaphore(name))

        def lanes(name):
            return [sem(f"{name}{q}") for q in range(LANES)]

        bank = [ctx.enter_context(nc.psum_tensor(f"bank{i}", [P, 512], F32)) for i in range(8)]

        res = sb("res", [P, NT, D])
        xt_hi = sb("xt_hi", [P, KD, B * T], F32R)
        xt_lo = sb("xt_lo", [P, KD, B * T], F32R)
        ident = sb("ident", [P, P])
        ones = sb("ones", [P, P])
        iota8 = sb("iota8", [P, E])
        neg_half = sb("neg_half", [P, 4])
        half = sb("half", [P, 4])
        euler = sb("euler", [P, TOPK * NT])
        gw_rows = sb("gw_rows", [E, D])
        gwt_hi = sb("gwt_hi", [P, KD, E], F32R)
        gwt_lo = sb("gwt_lo", [P, KD, E], F32R)
        logits_t = sb("logits_t", [E, B * T])
        logit_part = sb("logit_part", [E, B])
        logit_sum = sb("logit_sum", [E, 1])
        sum_row = sb("sum_row", [P, E])
        top_v = sb("top_v", [P, 8])
        top_i = sb("top_i", [P, 8], U32)
        top_f = sb("top_f", [P, 8])
        onehot = sb("onehot", [P, TOPK, E])
        picked = sb("picked", [P, NT, E])
        lk = sb("lk", [P, TOPK, NT])
        lmax = sb("lmax", [P, NT])
        lsub = sb("lsub", [P, TOPK, NT])
        lexp = sb("lexp", [P, TOPK, NT])
        lden = sb("lden", [P, NT])
        lrec = sb("lrec", [P, NT])
        rw = sb("rw", [P, PAIRS, NT])
        b1_rows = sb("b1_rows", [TOPK * GROUPS * FT, P])
        gelu_warm = sb("gelu_warm", [P, 1])
        b1_col = sb("b1_col", [P, TOPK * GROUPS * FT])

        early = ExitStack()

        def lane_sb(name, shape, dt=F32):
            return [sb(f"{name}{q}", shape, dt, early) for q in range(LANES)]

        wt = lane_sb("wt", [P, OT, D])
        cx = lane_sb("cx", [P, OT, I])
        xn = lane_sb("xn", [P, TT, D])
        xs = lane_sb("xs", [P, TT, D])
        ws = lane_sb("ws", [P, OT, D])
        xq = lane_sb("xq", [P, KD, T], BF16)
        wq = lane_sb("wq", [P, KD, O], BF16)
        av = lane_sb("av", [P, TT, I])
        wsc_row = lane_sb("wsc_row", [P, O])
        amax_x = lane_sb("amax_x", [P, D])
        amax_w = lane_sb("amax_w", [P, D])
        amax_c = lane_sb("amax_c", [P, I])
        stats = lane_sb("stats", [P, TT, 6])
        mv = lane_sb("mv", [P, TT, 2])
        var_e = lane_sb("var_e", [P, TT])
        rstd = lane_sb("rstd", [P, TT])
        nmean = lane_sb("nmean", [P, TT])
        nmr = lane_sb("nmr", [P, TT])
        cmax = lane_sb("cmax", [P, 2, KD])
        cclip = lane_sb("cclip", [P, 2, KD])
        crec = lane_sb("crec", [P, KD])
        ratio = lane_sb("ratio", [P, KD])
        sroot = lane_sb("sroot", [P, KD])
        smooth = lane_sb("smooth", [P, 2, KD])
        rmax = lane_sb("rmax", [P, 2, TT])
        scale = lane_sb("scale", [P, 2, TT])
        rscale = lane_sb("rscale", [P, 2, TT])
        early.close()

        raw1 = sb("raw1", [P, FT, KD, P])
        raw2 = sb("raw2", [P, FT, D])
        w1_hi = [sb(f"w1_hi{h}", [P, FT, KD, P], F32R) for h in range(2)]
        w1_lo = [sb(f"w1_lo{h}", [P, FT, KD, P], F32R) for h in range(2)]
        w2_hi = [sb(f"w2_hi{h}", [P, FT, D], F32R) for h in range(2)]
        w2_lo = [sb(f"w2_lo{h}", [P, FT, D], F32R) for h in range(2)]
        hid = [sb(f"hid{h}", [P, T]) for h in range(2)]
        h_hi = [sb(f"h_hi{h}", [P, T], F32R) for h in range(2)]
        h_lo = [sb(f"h_lo{h}", [P, T], F32R) for h in range(2)]
        b2_row = sb("b2_row", [P, TOPK, D])

        consts_ready = sem("consts_ready")
        own_wait = sem("own_wait")
        x_load = [sem(f"x_load{b}") for b in range(B)]
        wt_load = [sem(f"wt_load{b}") for b in range(B)]
        cx_load = [sem(f"cx_load{b}") for b in range(B)]
        gw_load = sem("gw_load")
        x_in, wt_in, cx_in = lanes("x_in"), lanes("wt_in"), lanes("cx_in")
        srow_ready, wmul_ready = lanes("srow_ready"), lanes("wmul_ready")
        a_ready, res_added = lanes("a_ready"), lanes("res_added")
        dve_link = sem("dve_link")
        pool_link = sem("pool_link")
        gwt_ps, gwt_ready = sem("gwt_ps"), sem("gwt_ready")
        var_ready, rstd_ready, nmr_ready = lanes("var_ready"), lanes("rstd_ready"), lanes("nmr_ready")
        xn_ready, xn2_ready = lanes("xn_ready"), lanes("xn2_ready")
        amaxw_ready, amaxx_ready = lanes("amaxw_ready"), lanes("amaxx_ready")
        amaxc_ready, amaxc_t = lanes("amaxc_ready"), lanes("amaxc_t")
        amaxw_t, amaxx_t = lanes("amaxw_t"), lanes("amaxx_t")
        ratio_ready, root_ready, smooth_ready = lanes("ratio_ready"), lanes("root_ready"), lanes("smooth_ready")
        smooth_rows = lanes("smooth_rows")
        xscale_ready, wscale_ready = lanes("xscale_ready"), lanes("wscale_ready")
        xr_ready, wr_ready = lanes("xr_ready"), lanes("wr_ready")
        xt_ps, wt_ps = lanes("xt_ps"), lanes("wt_ps")
        xq_ready, wq_ready = lanes("xq_ready"), lanes("wq_ready")
        wrow_ps, wrow_ready = lanes("wrow_ps"), lanes("wrow_ready")
        prod_ready = lanes("prod_ready")
        y_down = lanes("y_down")
        gu_ready, silu_ready = lanes("gu_ready"), lanes("silu_ready")
        xn2t_ps, hi_ready, lo_ready = lanes("xn2t_ps"), lanes("hi_ready"), lanes("lo_ready")
        logit_ps, logit_ready = lanes("logit_ps"), lanes("logit_ready")
        sum_ready, sumrow_ps, top_ready = sem("sum_ready"), sem("sumrow_ps"), sem("top_ready")
        logcol_ps, lsub_ready, lexp_ready = sem("logcol_ps"), sem("lsub_ready"), sem("lexp_ready")
        raw1_load = [sem(f"raw1_load{s}") for s in range(FT)]
        raw2_load = [sem(f"raw2_load{s}") for s in range(FT)]
        b1_load, b2_load = sem("b1_load"), sem("b2_load")
        b1_ps, b1_ready = sem("b1_ps"), sem("b1_ready")
        raw_in = sem("raw_in")
        w_hi_ready, w_ready = sem("w_hi_ready"), sem("w_ready")
        up_ready, hid_ready, h_ready = sem("up_ready"), sem("hid_ready"), sem("h_ready")
        y_ready, y_free = sem("y_ready"), sem("y_free")
        stored = sem("stored")

        MULS = 2 * OT
        up_bank, y_bank = bank[0:2], bank[4:8]
        STEPS = FT * B
        block = ctx.enter_context(nc.Block())

        @block.sync
        def _(sp):
            sp.dma_start(gw_rows[:, :], gate_w).then_inc(gw_load, 16)
            for r in range(ROUNDS):
                for q in range(LANES):
                    b = r * LANES + q
                    sp.dma_start(res[:, b * TT:(b + 1) * TT, :], x_v[b]).then_inc(x_load[b], 16)
                for q in range(LANES):
                    b = r * LANES + q
                    if r:
                        sp.wait_ge(wmul_ready[q], MULS * (r - 1) + OT)
                    sp.dma_start(wt[q][:, :, :], wt_v[b]).then_inc(wt_load[b], 16)
                for q in range(LANES):
                    b = r * LANES + q
                    if r:
                        sp.wait_ge(wmul_ready[q], MULS * r)
                    sp.dma_start(cx[q][:, :, :], cx_v[b]).then_inc(cx_load[b], 16)
                for load, ready in ((x_load, x_in), (wt_load, wt_in), (cx_load, cx_in)):
                    for q in range(LANES):
                        sp.wait_ge(load[r * LANES + q], 16)
                        sp.sem_inc(ready[q], 1)

            sp.wait_ge(top_ready, 1)
            def value_of(k):
                return sp.value_load(top_i[0:1, k:k + 1], min_val=0, max_val=E - 1)

            expert = [value_of(0)]

            def load_unit(e, u, s):
                sp.dma_start(raw1[:, s, :, :], w1_v[ds(e, 1), ds(u, 1)].rearrange("e u p k f -> (e u p) k f")
                             ).then_inc(raw1_load[s], 16)
                sp.dma_start(raw2[:, s, :], w2_v[ds(e, 1), ds(u, 1)].rearrange("e u f d -> (e u f) d")
                             ).then_inc(raw2_load[s], 16)

            for s in range(FT):
                load_unit(expert[0], s, s)
                if s == 1:
                    expert.append(value_of(1))
                    for k in range(TOPK):
                        sp.dma_start(b1_rows[k * GROUPS * FT:(k + 1) * GROUPS * FT, :],
                                     b1_v[ds(expert[k], 1)].rearrange("e u f -> (e u) f")).then_inc(b1_load, 16)
            for k in range(TOPK):
                sp.dma_start(b2_row[:, k, :], b2[ds(expert[k], 1), :].to_broadcast([P, D])).then_inc(b2_load, 16)
            for s in range(FT):
                sp.wait_ge(raw1_load[s], 16)
                sp.sem_inc(raw_in, 1)
                sp.wait_ge(raw2_load[s], 16)
                sp.sem_inc(raw_in, 1)
            for g in range(1, TOPK * GROUPS):
                for s in range(FT):
                    sp.wait_ge(w_ready, 2 * ((g - 1) * FT + s) + 2)
                    load_unit(expert[g // GROUPS], (g % GROUPS) * FT + s, s)
                    sp.wait_ge(raw1_load[s], 16 * (g + 1))
                    sp.sem_inc(raw_in, 1)
                    sp.wait_ge(raw2_load[s], 16 * (g + 1))
                    sp.sem_inc(raw_in, 1)
            before = TT + (TOPK * GROUPS - 1) * NT
            for b in range(B - 1):
                sp.wait_ge(y_free, before + (b + 1) * TT)
                sp.dma_start(out_v[b], res[:, b * TT:(b + 1) * TT, :]).then_inc(stored, 16)
            for j in range(TT):
                sp.wait_ge(y_free, before + (B - 1) * TT + j + 1)
                sp.dma_start(out_v[B - 1, :, j, :], res[:, (B - 1) * TT + j, :]).then_inc(stored, 16)
            sp.wait_ge(stored, 16 * (B - 1 + TT))

        @block.gpsimd
        def _(pool):
            g = nc.gpsimd
            g.memset(ident[:, :], 0.0).then_inc(pool_link, 1)
            g.memset(ones[:, :], 1.0)
            g.memset(half[:, :], 0.5)
            g.memset(neg_half[:, :], -0.5)
            g.memset(euler[:, :], EULER)
            g.iota(iota8[:, :], pattern=[[1, E]], base=0, channel_multiplier=0,
                   allow_small_or_imprecise_dtypes=True)
            pool.wait_ge(pool_link, 1)
            g.affine_select(out=ident[:, :], in_=ident[:, :], compare_op=ALU.not_equal, fill=1.0, base=0,
                            pattern=[[-1, P]], channel_multiplier=1).then_inc(consts_ready, 1)

            def root(q, i, c, n):
                pool.wait_ge(ratio_ready[q], 2 * i + c)
                g.tensor_tensor(sroot[q][:, 0:n], ratio[q][:, 0:n], half[:, 0:n], ALU.pow).then_inc(root_ready[q], 1)

            def smooth_weight(q, i, c, src, n):
                pool.wait_ge(srow_ready[q], 2 * i + c)
                for j in range(OT):
                    g.tensor_tensor(ws[q][:, j, 0:n], src[q][:, j, :], wsc_row[q][:, 0:n], ALU.mult
                                    ).then_inc(wmul_ready[q], 1)

            def gate_up_product(q, i):
                for j in range(TT):
                    pool.wait_ge(silu_ready[q], TT * i + j + 1)
                    g.tensor_tensor(av[q][:, j, :], av[q][:, j, :], xn[q][:, j, I:O], ALU.mult
                                    ).then_inc(a_ready[q], 1)

            def add_residual(q, i):
                for j in range(TT):
                    pool.wait_ge(y_down[q], TT * i + j + 1)
                    pool.sem_inc(own_wait, 1)
                    r = res[:, ds((LANES * i + q) * TT + j, 1), :].rearrange("p o d -> p (o d)")
                    g.tensor_tensor(r, r, xs[q][:, j, :], ALU.add).then_inc(res_added[q], 1)

            def round_weight(q, i, c, n):
                pool.wait_ge(wscale_ready[q], 2 * i + c)
                pool.sem_inc(own_wait, 1)
                for j in range(OT):
                    v = ws[q][:, j, 0:n]
                    g.tensor_scalar(v, v, rscale[q][:, 1, j:j + 1], ROUND, ALU.mult, ALU.add
                                    ).then_inc(wr_ready[q], 1)

            def inv_std(q, i, c):
                pool.wait_ge(var_ready[q], 2 * i + c)
                g.tensor_tensor(rstd[q][:, :], var_e[q][:, :], neg_half[:, :], ALU.pow).then_inc(rstd_ready[q], 1)
                pool.wait_ge(rstd_ready[q], 2 * i + c)
                g.tensor_tensor(nmr[q][:, :], nmean[q][:, :], rstd[q][:, :], ALU.mult).then_inc(nmr_ready[q], 1)

            with pool.Fori(0, ROUNDS) as i:
                for q in range(LANES):
                    inv_std(q, i, 1)
                for q in range(LANES):
                    root(q, i, 1, KD)
                for q in range(LANES):
                    smooth_weight(q, i, 1, wt, D)
                for q in range(LANES):
                    round_weight(q, i, 1, D)
                for q in range(LANES):
                    gate_up_product(q, i)
                for q in range(LANES):
                    root(q, i, 2, KI)
                for q in range(LANES):
                    smooth_weight(q, i, 2, cx, I)
                for q in range(LANES):
                    round_weight(q, i, 2, I)
                for q in range(LANES):
                    add_residual(q, i)
                for q in range(LANES):
                    inv_std(q, i, 2)
            pool.wait_ge(lsub_ready, TOPK)
            g.tensor_tensor(lexp[:, :, :].rearrange("p k n -> p (k n)"), euler[:, :],
                            lsub[:, :, :].rearrange("p k n -> p (k n)"), ALU.pow).then_inc(lexp_ready, 1)

        @block.tensor
        def _(pe):
            t = nc.tensor

            def bk(q, k):
                return bank[4 * q + k]

            pe.wait_ge(consts_ready, 1)
            pe.wait_ge(gw_load, 16)
            for k in range(KD):
                last = t.transpose(bank[0][:, k * E:(k + 1) * E], gw_rows[:, k * P:(k + 1) * P], ident[0:E, 0:E])
            last.then_inc(gwt_ps, 1)

            def transpose_wmax(q, i):
                pe.wait_ge(amaxw_ready[q], i + 1)
                if q == 0:
                    pe.wait_ge(gwt_ready, 1)
                for k in range(KD):
                    last = t.transpose(bk(q, 0)[:, k * P:(k + 1) * P], amax_w[q][:, k * P:(k + 1) * P], ident[:, :])
                last.then_inc(amaxw_t[q], 1)

            def transpose_cmax(q, i):
                pe.wait_ge(amaxc_ready[q], i + 1)
                for k in range(KI):
                    last = t.transpose(bk(q, 1)[:, k * P:(k + 1) * P], amax_c[q][:, k * P:(k + 1) * P], ident[:, :])
                last.then_inc(amaxc_t[q], 1)

            def transpose_xmax(q, i, c, n, to):
                pe.wait_ge(amaxx_ready[q], 2 * i + c)
                for k in range(n):
                    last = t.transpose(bk(q, to)[:, k * P:(k + 1) * P], amax_x[q][:, k * P:(k + 1) * P], ident[:, :])
                last.then_inc(amaxx_t[q], 1)

            def spread(dst, col):
                return t.matmul(dst, col.to_broadcast([P, P]), ident[:, :], start=True, stop=True)

            def smooth_to_rows(q, i, c, n, to):
                pe.wait_ge(smooth_ready[q], 2 * i + c)
                for w in range(2):
                    b, o = to[w]
                    for k in range(n):
                        last = spread(bk(q, b)[:, o + k * P:o + (k + 1) * P], smooth[q][:, w, k:k + 1])
                    last.then_inc(smooth_rows[q], 1)

            def transpose_x(q, i, c, n, to):
                for k in range(n):
                    for j in range(TT):
                        if k == 0:
                            pe.wait_ge(xr_ready[q], 2 * TT * i + TT * (c - 1) + j + 1)
                        last = t.transpose(bk(q, to[k])[:, j * P:(j + 1) * P], xs[q][:, j, k * P:(k + 1) * P],
                                           ident[:, :])
                    last.then_inc(xt_ps[q], 1)

            def transpose_w(q, i, c, n, to, free):
                for k in range(n):
                    if free is not None:
                        free(k)
                    for j in range(OT):
                        if k == 0:
                            pe.wait_ge(wr_ready[q], 2 * OT * i + OT * (c - 1) + j + 1)
                        last = t.transpose(bk(q, to[k])[:, j * P:(j + 1) * P], ws[q][:, j, k * P:(k + 1) * P],
                                           ident[:, :])
                    last.then_inc(wt_ps[q], 1)

            def scales_to_row(q, i, c, to):
                pe.wait_ge(wscale_ready[q], 2 * i + c)
                for j in range(OT):
                    last = spread(bk(q, to)[:, j * P:(j + 1) * P], scale[q][:, 1, j:j + 1])
                last.then_inc(wrow_ps[q], 1)

            NQ = KD + KI

            def product(q, i, c, n):
                done = NQ * i + (KD if c == 1 else NQ)
                pe.wait_ge(xq_ready[q], done)
                pe.wait_ge(wq_ready[q], done)
                pe.wait_ge(wrow_ready[q], 2 * i + c)
                for j in range(TT):
                    for k in range(n):
                        last = t.matmul(bk(q, j)[:, 0:O], xq[q][:, k, j * P:(j + 1) * P], wq[q][:, k, :],
                                        start=(k == 0), stop=(k == n - 1))
                    last.then_inc(prod_ready[q], 1)

            def transpose_xn2(q, i):
                for k in range(KD):
                    for j in range(TT):
                        if k == 0:
                            pe.wait_ge(xn2_ready[q], TT * i + j + 1)
                        last = t.transpose(bk(q, k)[:, j * P:(j + 1) * P], xn[q][:, j, k * P:(k + 1) * P],
                                           ident[:, :])
                    last.then_inc(xn2t_ps[q], 1)

            def router(q, i):
                pe.wait_ge(lo_ready[q], KD * i + KD)
                at = (LANES * i + q) * T
                n = 0
                for k in range(KD):
                    for a, v in ((gwt_hi, xt_hi), (gwt_hi, xt_lo), (gwt_lo, xt_hi)):
                        last = t.matmul(bk(q, 3)[0:E, :], a[:, k, :], v[:, k, ds(at, T)],
                                        start=(n == 0), stop=(n == 3 * KD - 1))
                        n += 1
                last.then_inc(logit_ps[q], 1)

            with pe.Fori(0, ROUNDS) as i:
                for q in range(LANES):
                    transpose_wmax(q, i)
                for q in range(LANES):
                    transpose_xmax(q, i, 1, KD, 2)
                for q in range(LANES):
                    smooth_to_rows(q, i, 1, KD, ((2, 0), (3, 0)))
                for q in range(LANES):
                    transpose_x(q, i, 1, KD, (0, 1, 2, 3))
                for q in range(LANES):
                    pe.wait_ge(xq_ready[q], NQ * i + 1)
                    scales_to_row(q, i, 1, 0)

                    def free(k, q=q):
                        if k < KD - 1:
                            pe.wait_ge(xq_ready[q], NQ * i + k + 2)
                        else:
                            pe.wait_ge(wrow_ready[q], 2 * i + 1)
                    transpose_w(q, i, 1, KD, (1, 2, 3, 0), free)
                for q in range(LANES):
                    product(q, i, 1, KD)
                for q in range(LANES):
                    pe.wait_ge(gu_ready[q], TT * i + 2)
                    transpose_cmax(q, i)
                for q in range(LANES):
                    transpose_xmax(q, i, 2, KI, 0)
                for q in range(LANES):
                    smooth_to_rows(q, i, 2, KI, ((1, 0), (0, 0)))
                for q in range(LANES):
                    transpose_x(q, i, 2, KI, (2, 3))
                for q in range(LANES):
                    transpose_w(q, i, 2, KI, (0, 1), None)
                    pe.wait_ge(xq_ready[q], NQ * i + KD + 1)
                    scales_to_row(q, i, 2, 2)
                for q in range(LANES):
                    product(q, i, 2, KI)
                for q in range(LANES):
                    transpose_xn2(q, i)
                for q in range(LANES):
                    router(q, i)

            pe.wait_ge(sum_ready, 1)
            t.matmul(bank[1][:, 0:E], logit_sum[:, 0:1].to_broadcast([E, P]), ident[0:E, 0:E],
                     start=True, stop=True).then_inc(sumrow_ps, 1)
            for n in range(NT):
                last = t.transpose(bank[3][:, n * E:(n + 1) * E], logits_t[:, n * P:(n + 1) * P], ident[0:E, 0:E])
            last.then_inc(logcol_ps, 1)

            def up(group, h, f, at):
                pe.wait_ge(w_ready, 2 * (group * FT + f) + 1)
                n = 0
                for k in range(KD):
                    for a, v in ((w1_hi, xt_hi), (w1_hi, xt_lo), (w1_lo, xt_hi)):
                        last = t.matmul(up_bank[f % 2][:, :], a[h][:, f, k, :], v[:, k, ds(at, T)],
                                        start=(n == 0), stop=(n == 3 * KD - 1))
                        n += 1
                last.then_inc(up_ready, 1)

            def down(group, h, f, b):
                pe.wait_ge(w_ready, 2 * (group * FT + f) + 2)
                pe.wait_ge(h_ready, group * STEPS + b * FT + f + 1)
                for j in range(TT):
                    if f == 0:
                        pe.wait_ge(y_free, group * NT + b * TT + j + 1)
                    n = 0
                    for a, v in ((h_hi, w2_hi), (h_hi, w2_lo), (h_lo, w2_hi)):
                        last = t.matmul(y_bank[j][:, :], a[f % 2][:, j * P:(j + 1) * P], v[h][:, f, :],
                                        start=(f == 0 and n == 0), stop=(f == FT - 1 and n == 2),
                                        skip_group_check=True)
                        n += 1
                    if f == FT - 1:
                        last.then_inc(y_ready, 1)

            def pair_of_groups(p, final):
                for h in range(2):
                    group = 2 * p + h
                    with pe.Fori(0, B - 1) as b:
                        for f in range(FT):
                            if f < FT - 1:
                                up(group, h, f + 1, b * T)
                            else:
                                up(group, h, 0, b * T + T)
                            down(group, h, f, b)
                    for f in range(FT):
                        if f < FT - 1:
                            up(group, h, f + 1, (B - 1) * T)
                        elif not (final and h):
                            up(group + 1, 1 - h, 0, 0)
                        down(group, h, f, B - 1)

            up(0, 0, 0, 0)
            pe.wait_ge(b1_load, 16 * TOPK)
            t.transpose(bank[2][:, 0:TOPK * GROUPS * FT], b1_rows[:, :],
                        ident[0:TOPK * GROUPS * FT, 0:TOPK * GROUPS * FT]).then_inc(b1_ps, 1)
            with pe.Fori(0, PAIRS - 1) as p:
                pair_of_groups(p, False)
            pair_of_groups(PAIRS - 1, True)

        @block.scalar
        def _(act):
            s = nc.scalar

            def bk(q, k):
                return bank[4 * q + k]

            def normalise(q, i):
                act.wait_ge(nmr_ready[q], 2 * i + 1)
                act.sem_inc(own_wait, 1)
                b = LANES * i + q
                for j in range(TT):
                    s.activation(xn[q][:, j, :], res[:, ds(b * TT + j, 1), :].rearrange("p o d -> p (o d)"),
                                 ACT.Identity, bias=nmr[q][:, j:j + 1], scale=rstd[q][:, j:j + 1]
                                 ).then_inc(xn_ready[q], 1)

            def keep_smooth_row(q, i, c, n, frm):
                act.wait_ge(smooth_rows[q], 4 * i + 2 * c)
                s.copy(wsc_row[q][:, 0:n], bk(q, frm)[:, 0:n]).then_inc(srow_ready[q], 1)

            def round_x(q, i, c, n):
                act.wait_ge(xscale_ready[q], 2 * i + c)
                for j in range(TT):
                    v = xs[q][:, j, 0:n]
                    s.activation(v, v, ACT.Copy, bias=ROUND, scale=rscale[q][:, 0, j:j + 1]
                                 ).then_inc(xr_ready[q], 1)

            NQ = KD + KI

            def integers_x(q, i, c, n, frm):
                for k in range(n):
                    act.wait_ge(xt_ps[q], NQ * i + (c - 1) * KD + k + 1)
                    s.activation(xq[q][:, k, :], bk(q, frm[k])[:, :], ACT.Copy, bias=-ROUND).then_inc(xq_ready[q], 1)

            def keep_scale_row(q, i, c, frm):
                act.wait_ge(wrow_ps[q], 2 * i + c)
                s.copy(wsc_row[q][:, :], bk(q, frm)[:, :]).then_inc(wrow_ready[q], 1)

            with act.Fori(0, ROUNDS) as i:
                for q in range(LANES):
                    normalise(q, i)
                for q in range(LANES):
                    keep_smooth_row(q, i, 1, D, 3)
                for q in range(LANES):
                    round_x(q, i, 1, D)
                for q in range(LANES):
                    integers_x(q, i, 1, KD, (0, 1, 2, 3))
                    keep_scale_row(q, i, 1, 0)
                for q in range(LANES):
                    for j in range(TT):
                        act.wait_ge(gu_ready[q], TT * i + j + 1)
                        s.activation(av[q][:, j, :], xn[q][:, j, 0:I], ACT.Silu).then_inc(silu_ready[q], 1)
                for q in range(LANES):
                    keep_smooth_row(q, i, 2, I, 0)
                for q in range(LANES):
                    round_x(q, i, 2, I)
                for q in range(LANES):
                    integers_x(q, i, 2, KI, (2, 3))
                    keep_scale_row(q, i, 2, 2)
                for q in range(LANES):
                    at = (LANES * i + q) * T
                    for k in range(KD):
                        act.wait_ge(xn2t_ps[q], KD * i + k + 1)
                        s.copy(xt_hi[:, k, ds(at, T)], bk(q, k)[:, :]).then_inc(hi_ready[q], 1)
                for q in range(LANES):
                    act.wait_ge(logit_ps[q], i + 1)
                    b = LANES * i + q
                    s.activation(logits_t[:, ds(b * T, T)], bk(q, 3)[0:E, :], ACT.Copy,
                                 accum_out=logit_part[:, ds(b, 1)]).then_inc(logit_ready[q], 1)

            def split_hi(n, w1_at, w2_at):
                act.wait_ge(raw1_load[n], 16)
                s.copy(w1_at[1], w1_at[0]).then_inc(w_hi_ready, 1)
                act.wait_ge(raw2_load[n], 16)
                s.copy(w2_at[1], w2_at[0]).then_inc(w_hi_ready, 1)

            act.wait_ge(consts_ready, 1)
            s.activation(gelu_warm[:, :], half[:, 0:1], ACT.Gelu_apprx_tanh)
            for f in range(FT):
                split_hi(f, (raw1[:, f], w1_hi[0][:, f]), (raw2[:, f], w2_hi[0][:, f]))
            act.wait_ge(b1_ps, 1)
            s.copy(b1_col[:, :], bank[2][:, 0:TOPK * GROUPS * FT]).then_inc(b1_ready, 1)
            act.wait_ge(b1_ready, 1)

            def pair_of_groups(p, final):
                for h in range(2):
                    group = 2 * p + h
                    with act.Fori(0, B) as b:
                        for f in range(FT):
                            act.wait_ge(up_ready, group * STEPS + b * FT + f + 1)
                            col = group * FT + f
                            bias = b1_col[:, ds(col, 1)]
                            s.activation(hid[f % 2][:, :], up_bank[f % 2][:, :], ACT.Gelu_apprx_tanh,
                                         bias=bias).then_inc(hid_ready, 1)
                            s.activation(h_hi[f % 2][:, :], up_bank[f % 2][:, :], ACT.Gelu_apprx_tanh,
                                         bias=bias).then_inc(hid_ready, 1)
                            nxt = 1 - h
                            if f == 2 and not (final and h):
                                n = (group + 1) * FT + b
                                act.wait_ge(raw_in, 2 * n + 2)
                                s.copy(w1_hi[nxt][:, ds(b, 1)], raw1[:, ds(b, 1)]).then_inc(w_hi_ready, 1)
                                s.copy(w2_hi[nxt][:, ds(b, 1)], raw2[:, ds(b, 1)]).then_inc(w_hi_ready, 1)

            with act.Fori(0, PAIRS - 1) as p:
                pair_of_groups(p, False)
            pair_of_groups(PAIRS - 1, True)

        @block.vector
        def _(dve):
            v = nc.vector

            def bk(q, k):
                return bank[4 * q + k]

            chain = [0, 0]

            def link(ins):
                chain[0] += 1
                ins.then_inc(dve_link, 1)
                dve.wait_ge(dve_link, chain[1] + chain[0])

            dve.wait_ge(gwt_ps, 1)
            g_ps = bank[0][:, 0:KD * E].rearrange("p (k e) -> p k e", e=E)
            link(v.tensor_copy(gwt_hi[:, :, :], g_ps))
            v.tensor_tensor(gwt_lo[:, :, :], g_ps, gwt_hi[:, :, :].bitcast(F32), ALU.subtract).then_inc(gwt_ready, 1)

            def moments(q, i, c):
                b = LANES * i + q
                dve.sem_inc(own_wait, 1)
                for j in range(TT):
                    if c == 2:
                        dve.wait_ge(res_added[q], TT * i + j + 1)
                        dve.sem_inc(own_wait, 1)
                    ins = v.bn_stats(stats[q][:, j, :], res[:, ds(b * TT + j, 1), :].rearrange("p o d -> p (o d)"))
                link(ins)
                dve.sem_inc(own_wait, 1)
                for j in range(TT):
                    ins = v.bn_aggr(mv[q][:, j, :], stats[q][:, j, :])
                link(ins)
                v.tensor_scalar(nmean[q][:, :], mv[q][:, :, 0], -1.0, None, ALU.mult)
                v.tensor_scalar(var_e[q][:, :], mv[q][:, :, 1], LN_EPS, None, ALU.add).then_inc(var_ready[q], 1)

            def abs_max(dst, src):
                return v.tensor_reduce(dst, src, AX.X, ALU.max, apply_absolute_value=True)

            def smoothing(q, i, c, n, act_bank):
                dve.wait_ge(amaxx_t[q], 2 * i + c)
                link(v.tensor_reduce(cmax[q][:, 0, 0:n],
                                     bk(q, act_bank)[:, 0:n * P].rearrange("p (k t) -> p k t", t=P), AX.X, ALU.max))
                link(v.tensor_scalar(cclip[q][:, :, 0:n], cmax[q][:, :, 0:n], QEPS, None, ALU.max))
                link(v.reciprocal(crec[q][:, 0:n], cclip[q][:, 1, 0:n]))
                v.tensor_tensor(ratio[q][:, 0:n], cclip[q][:, 0, 0:n], crec[q][:, 0:n], ALU.mult
                                ).then_inc(ratio_ready[q], 1)

            def inverse(q, i, c, n):
                dve.wait_ge(root_ready[q], 2 * i + c)
                link(v.tensor_scalar(smooth[q][:, 1, 0:n], sroot[q][:, 0:n], QEPS, None, ALU.max))
                v.reciprocal(smooth[q][:, 0, 0:n], smooth[q][:, 1, 0:n]).then_inc(smooth_ready[q], 1)

            def row_scales(q, m, w, n, ready):
                link(abs_max(rmax[q][:, w, :], m[q][:, :, 0:n]))
                link(v.tensor_scalar(scale[q][:, w, :], rmax[q][:, w, :], QEPS, 1.0 / QMAX, ALU.max, ALU.mult))
                v.reciprocal(rscale[q][:, w, :], scale[q][:, w, :]).then_inc(ready[q], 1)

            def smooth_x(q, i, c, n, src, frm):
                dve.wait_ge(smooth_rows[q], 4 * i + 2 * c - 1)
                row = bk(q, frm)[:, 0:n].rearrange("p (o n) -> p o n", o=1).to_broadcast([P, TT, n])
                link(v.tensor_tensor(xs[q][:, :, 0:n], src[q][:, :, :], row, ALU.mult))
                row_scales(q, xs, 0, n, xscale_ready)

            def scale_w(q, i, c, n):
                dve.wait_ge(wmul_ready[q], MULS * i + OT * c)
                row_scales(q, ws, 1, n, wscale_ready)

            def amax_ctx(q, i):
                dve.wait_ge(cx_in[q], i + 1)
                v.tensor_reduce(amax_c[q][:, :], cx[q][:, :, :].rearrange("p j d -> p d j"), AX.X, ALU.max,
                                apply_absolute_value=True).then_inc(amaxc_ready[q], 1)

            NQ = KD + KI

            def integers_w(q, i, c, n, frm):
                for k in range(n):
                    dve.wait_ge(wt_ps[q], NQ * i + (c - 1) * KD + k + 1)
                    v.tensor_scalar(wq[q][:, k, :], bk(q, frm[k])[:, :], -ROUND, None, ALU.add
                                    ).then_inc(wq_ready[q], 1)

            def dequant(q, i, c, dst, ready):
                dve.wait_ge(wrow_ready[q], 2 * i + c)
                for j in range(TT):
                    dve.wait_ge(prod_ready[q], 2 * TT * i + TT * (c - 1) + j + 1)
                    ins = v.scalar_tensor_tensor(out=dst[:, j, :], in0=bk(q, j)[:, :],
                                                 scalar=scale[q][:, 0, j:j + 1], in1=wsc_row[q][:, :],
                                                 op0=ALU.mult, op1=ALU.mult)
                    ins.then_inc(ready, 1)

            with dve.Fori(0, ROUNDS) as i:
                chain[:] = [0, LINKS * i + 1]
                for q in range(LANES):
                    dve.wait_ge(x_in[q], i + 1)
                    moments(q, i, 1)
                for q in range(LANES):
                    dve.wait_ge(wt_in[q], i + 1)
                    v.tensor_reduce(amax_w[q][:, :], wt[q][:, :, :].rearrange("p j d -> p d j"), AX.X, ALU.max,
                                    apply_absolute_value=True).then_inc(amaxw_ready[q], 1)
                for q in range(LANES):
                    dve.wait_ge(xn_ready[q], TT * i + TT)
                    v.tensor_reduce(amax_x[q][:, :], xn[q][:, :, :].rearrange("p j d -> p d j"), AX.X, ALU.max,
                                    apply_absolute_value=True).then_inc(amaxx_ready[q], 1)
                    dve.wait_ge(amaxw_t[q], i + 1)
                    v.tensor_reduce(cmax[q][:, 1, :], bk(q, 0)[:, :].rearrange("p (k t) -> p k t", t=P),
                                    AX.X, ALU.max)
                for q in range(LANES):
                    smoothing(q, i, 1, KD, 2)
                for q in range(LANES):
                    inverse(q, i, 1, KD)
                amax_ctx(0, i)
                for q in range(LANES):
                    smooth_x(q, i, 1, D, xn, 2)
                for q in range(LANES):
                    scale_w(q, i, 1, D)
                amax_ctx(1, i)
                for q in range(LANES):
                    integers_w(q, i, 1, KD, (1, 2, 3, 0))
                for q in range(LANES):
                    dequant(q, i, 1, xn[q], gu_ready[q])
                for q in range(LANES):
                    dve.wait_ge(amaxc_t[q], i + 1)
                    v.tensor_reduce(cmax[q][:, 1, 0:KI], bk(q, 1)[:, 0:I].rearrange("p (k t) -> p k t", t=P),
                                    AX.X, ALU.max)
                    dve.wait_ge(a_ready[q], TT * i + TT)
                    v.tensor_reduce(amax_x[q][:, 0:I], av[q][:, :, :].rearrange("p j d -> p d j"), AX.X, ALU.max,
                                    apply_absolute_value=True).then_inc(amaxx_ready[q], 1)
                for q in range(LANES):
                    smoothing(q, i, 2, KI, 0)
                for q in range(LANES):
                    inverse(q, i, 2, KI)
                for q in range(LANES):
                    smooth_x(q, i, 2, I, av, 1)
                for q in range(LANES):
                    scale_w(q, i, 2, I)
                for q in range(LANES):
                    integers_w(q, i, 2, KI, (0, 1))
                for q in range(LANES):
                    dequant(q, i, 2, xs[q], y_down[q])
                for q in range(LANES):
                    moments(q, i, 2)
                for q in range(LANES):
                    dve.wait_ge(nmr_ready[q], 2 * i + 2)
                    for j in range(TT):
                        v.tensor_scalar(xn[q][:, j, :], res[:, ds((LANES * i + q) * TT + j, 1), :]
                                        .rearrange("p o d -> p (o d)"), mv[q][:, j, 0:1], rstd[q][:, j:j + 1],
                                        ALU.subtract, ALU.mult).then_inc(xn2_ready[q], 1)
                for q in range(LANES):
                    at = (LANES * i + q) * T
                    for k in range(KD):
                        dve.wait_ge(hi_ready[q], KD * i + k + 1)
                        v.tensor_tensor(xt_lo[:, k, ds(at, T)], bk(q, k)[:, :],
                                        xt_hi[:, k, ds(at, T)].bitcast(F32), ALU.subtract
                                        ).then_inc(lo_ready[q], 1)
                assert chain[0] == LINKS, chain[0]
            chain[:] = [0, LINKS * ROUNDS + 1]

            for q in range(LANES):
                dve.wait_ge(logit_ready[q], ROUNDS)
            dve.sem_inc(y_free, TT)
            v.tensor_reduce(logit_sum[:, :], logit_part[:, :], AX.X, ALU.add).then_inc(sum_ready, 1)
            dve.wait_ge(sumrow_ps, 1)
            link(v.tensor_copy(sum_row[:, :], bank[1][:, 0:E]))
            link(v.max(top_v[:, :], sum_row[:, :]))
            v.max_index(top_i[:, :], top_v[:, :], sum_row[:, :]).then_inc(top_ready, 1)
            dve.wait_ge(top_ready, 1)

            link(v.tensor_copy(top_f[:, :], top_i[:, :]))
            for k in range(TOPK):
                link(v.tensor_scalar(onehot[:, k, :], iota8[:, :], top_f[:, k:k + 1], None, ALU.is_equal))
            dve.wait_ge(logcol_ps, 1)
            cols = bank[3][:, 0:NT * E].rearrange("p (n e) -> p n e", e=E)
            for k in range(TOPK):
                link(v.tensor_tensor(picked[:, :, :], cols,
                                     onehot[:, k:k + 1, :].to_broadcast([P, NT, E]), ALU.mult))
                link(v.tensor_reduce(lk[:, k, :], picked[:, :, :], AX.X, ALU.add))
            link(v.tensor_tensor(lmax[:, :], lk[:, 0, :], lk[:, 1, :], ALU.max))
            for k in range(TOPK):
                v.tensor_tensor(lsub[:, k, :], lk[:, k, :], lmax[:, :], ALU.subtract).then_inc(lsub_ready, 1)

            def split_lo(n, w1_at, w2_at):
                dve.wait_ge(w_hi_ready, 2 * n + 1)
                v.tensor_tensor(w1_at[2], w1_at[0], w1_at[1].bitcast(F32), ALU.subtract).then_inc(w_ready, 1)
                dve.wait_ge(w_hi_ready, 2 * n + 2)
                v.tensor_tensor(w2_at[2], w2_at[0], w2_at[1].bitcast(F32), ALU.subtract).then_inc(w_ready, 1)

            for f in range(FT):
                split_lo(f, (raw1[:, f], w1_hi[0][:, f], w1_lo[0][:, f]), (raw2[:, f], w2_hi[0][:, f], w2_lo[0][:, f]))
            dve.wait_ge(lexp_ready, 1)
            link(v.tensor_tensor(lden[:, :], lexp[:, 0, :], lexp[:, 1, :], ALU.add))
            link(v.reciprocal(lrec[:, :], lden[:, :]))
            for p in range(PAIRS):
                ins = v.tensor_tensor(rw[:, p, :], lexp[:, p * TOPK // PAIRS, :], lrec[:, :], ALU.mult)
            link(ins)

            def pair_of_groups(p, final):
                for h in range(2):
                    group = 2 * p + h
                    last_group = final and h == 1
                    with dve.Fori(0, B) as b:
                        for f in range(FT):
                            step = group * STEPS + b * FT + f
                            dve.wait_ge(hid_ready, 2 * step + 2)
                            v.tensor_tensor(h_lo[f % 2][:, :], hid[f % 2][:, :], h_hi[f % 2][:, :].bitcast(F32),
                                            ALU.subtract).then_inc(h_ready, 1)
                            nxt = 1 - h
                            if f == 2 and not last_group:
                                n = (group + 1) * FT + b
                                dve.wait_ge(w_hi_ready, 2 * n + 2)
                                v.tensor_tensor(w1_lo[nxt][:, ds(b, 1)], raw1[:, ds(b, 1)],
                                                w1_hi[nxt][:, ds(b, 1)].bitcast(F32), ALU.subtract
                                                ).then_inc(w_ready, 1)
                                v.tensor_tensor(w2_lo[nxt][:, ds(b, 1)], raw2[:, ds(b, 1)],
                                                w2_hi[nxt][:, ds(b, 1)].bitcast(F32), ALU.subtract
                                                ).then_inc(w_ready, 1)
                            if last_group and f < TOPK:
                                for j in range(TT):
                                    k = f
                                    r = res[:, ds(b * TT + j, 1), :].rearrange("p o d -> p (o d)")
                                    ins = v.scalar_tensor_tensor(
                                        out=r, in0=b2_row[:, k, :], scalar=rw[:, k * (PAIRS // TOPK), ds(b * TT + j, 1)],
                                        in1=r, op0=ALU.mult, op1=ALU.add)
                                ins.then_inc(dve_link, 1)
                                dve.wait_ge(dve_link, chain[1] + chain[0] + TOPK * b + f + 1)
                        for j in range(TT):
                            dve.wait_ge(y_ready, group * NT + b * TT + j + 1)
                            r = res[:, ds(b * TT + j, 1), :].rearrange("p o d -> p (o d)")
                            ins = v.scalar_tensor_tensor(
                                out=r, in0=y_bank[j][:, :], scalar=rw[:, p, ds(b * TT + j, 1)] if final else
                                rw[:, ds(p, 1), ds(b * TT + j, 1)].rearrange("p a b -> p (a b)"),
                                in1=r, op0=ALU.mult, op1=ALU.add)
                            ins.then_inc(y_free, 1)

            dve.wait_ge(b2_load, 16 * TOPK)
            with dve.Fori(0, PAIRS - 1) as p:
                pair_of_groups(p, False)
            pair_of_groups(PAIRS - 1, True)


LINKS = 44

_INS = ["x", "fside_BxS2xS2_0", "ctx_1024", "L0_ffn_gate_w", "L0_ffn_w1", "L0_ffn_b1", "L0_ffn_w2", "L0_ffn_b2"]
_OUT = (4, 512, 512)


def kernel(**inputs):
    import numpy as np
    import concourse.bacc as bacc
    from concourse.bass_utils import run_bass_kernel_spmd

    nc = bacc.Bacc("TRN2", target_bir_lowering=False, num_devices=1, dynamic_dma_scratch_size=1024)
    arrays, args = {}, []
    for name in _INS:
        a = np.ascontiguousarray(inputs[name])
        arrays[f"in_{name}"] = a
        args.append(nc.dram_tensor(f"in_{name}", a.shape, mybir.dt.from_np(a.dtype), kind="ExternalInput").ap())
    args.append(nc.dram_tensor("out_x", _OUT, F32, kind="ExternalOutput").ap())
    xattn_ffn(nc, *args)
    r = run_bass_kernel_spmd(nc, [arrays], core_ids=[0])
    return r.results[0]["out_x"]
```
